# Optimizing a Trainium2 kernel written in Bass

```python
import numpy as np
import jax
import jax.numpy as jnp

def _softmax(x, axis=-1):
    return jax.nn.softmax(x, axis=axis)

def _gelu(x):
    return jax.nn.gelu(x, approximate=True)

def _silu(x):
    return jax.nn.silu(x)

def _sigmoid(x):
    return jax.nn.sigmoid(x)

def _layernorm(x, axis=-1, eps=1e-05):
    m = jnp.mean(x, axis=axis, keepdims=True)
    v = jnp.var(x, axis=axis, keepdims=True)
    return (x - m) / jnp.sqrt(v + eps)

def _scatter_add(tgt, idx, src, axis=0):
    return tgt.at[idx].add(src)

def _segment_sum(src, seg, n):
    return jax.ops.segment_sum(src, seg, n)
kernel_name = 'mk_gnn_ffn_d1_gnn_r32_be9f9b'

def setup_inputs(seed: int=0):
    np.random.seed(seed)
    _w = jnp.asarray

    def _rec_inputs():
        import jax
        import jax.numpy as jnp
        _gk = jax.random.key(seed)
        x = -0.0005963 + 1.001 * jax.random.normal(jax.random.fold_in(_gk, 1), (96, 1024), jnp.float32)
        src = jax.random.randint(jax.random.fold_in(_gk, 2), (3072,), 0, 96, jnp.int32)
        dst = jax.random.randint(jax.random.fold_in(_gk, 3), (3072,), 0, 96, jnp.int32)
        _o = jnp.argsort(dst, stable=True)
        src = src[_o]
        dst = dst[_o]
        edge_type_5 = jax.random.randint(jax.random.fold_in(_gk, 12), (3072,), 0, 5, jnp.int32)
        return (x, src, dst, edge_type_5)
    x, src, dst, edge_type_5 = _rec_inputs()

    def _L0_gnn_setup():
        import jax, jax.numpy as jnp
        import numpy as np
        N = 96
        E = 3072
        IN_F = 1024
        OUT_F = 1024
        H = 16
        D = OUT_F // H
        NUM_ETYPES = 4

        def _build_mask(edge_index, edge_type, edge_type_weights, dtype):
            src, dst = (edge_index[0], edge_index[1])
            w = jax.nn.softplus(edge_type_weights)
            mask = jnp.full((N, N), -jnp.inf, dtype=dtype)
            mask = mask.at[src, dst].set(w[edge_type - 1])
            diag = jnp.diagonal(mask)
            idx = jnp.arange(N)
            mask = mask.at[idx, idx].set(jnp.where(jnp.isneginf(diag), w[3], diag))
            return mask
        key = jax.random.key(seed)
        ks = jax.random.split(key, 20)
        p = lambda k, shape: jax.random.normal(k, shape, dtype=jnp.float32) * 0.02
        return {'x': jax.random.normal(ks[0], (N, IN_F), dtype=jnp.float32), 'edge_index': jax.random.randint(ks[1], (2, E), 0, N), 'edge_type': jax.random.randint(ks[2], (E,), 1, NUM_ETYPES + 1), 'edge_type_weights': jnp.ones((NUM_ETYPES,), jnp.float32) + 0.1 * jax.random.normal(ks[3], (NUM_ETYPES,), dtype=jnp.float32), 'wq': p(ks[4], (OUT_F, IN_F)), 'bq': p(ks[5], (OUT_F,)), 'wk': p(ks[6], (OUT_F, IN_F)), 'bk': p(ks[7], (OUT_F,)), 'wv': p(ks[8], (OUT_F, IN_F)), 'bv': p(ks[9], (OUT_F,)), 'wiq': p(ks[10], (OUT_F, OUT_F)), 'biq': p(ks[11], (OUT_F,)), 'wik': p(ks[12], (OUT_F, OUT_F)), 'bik': p(ks[13], (OUT_F,)), 'wiv': p(ks[14], (OUT_F, OUT_F)), 'biv': p(ks[15], (OUT_F,)), 'wo': p(ks[16], (OUT_F, OUT_F)), 'bo': p(ks[17], (OUT_F,))}
    _L0_gnn_all = _L0_gnn_setup()
    _L0_gnn_in = {k: v for k, v in _L0_gnn_all.items() if k in ('edge_type_weights', 'wq', 'bq', 'wk', 'bk', 'wv', 'bv', 'wiq', 'biq', 'wik', 'bik', 'wiv', 'biv', 'wo', 'bo')}
    del _L0_gnn_all

    def _L0_ffn_setup():
        import jax, jax.numpy as jnp
        import numpy as np
        B, S, D_IN, D_OUT = (16, 128, 1024, 1024)
        ACT_BITS = 8
        QB = float(2 ** (ACT_BITS - 1) - 1)
        key = jax.random.key(seed)
        k1, k2, k3 = jax.random.split(key, 3)
        x = jax.random.normal(k1, (B, S, D_IN), dtype=jnp.float32)
        ternary_weight = jax.random.randint(k2, (D_OUT, D_IN), 0, 3, dtype=jnp.int32)
        bias = jax.random.normal(k3, (D_OUT,), dtype=jnp.float32)
        act_scale = (jnp.max(jnp.abs(x)) / QB).astype(jnp.float32)
        return {'x': x, 'ternary_weight': ternary_weight, 'bias': bias, 'act_scale': act_scale}
    _L0_ffn_all = _L0_ffn_setup()
    _L0_ffn_in = {k: v for k, v in _L0_ffn_all.items() if k in ('ternary_weight', 'bias', 'act_scale')}
    del _L0_ffn_all
    return {'x': x, 'src': src, 'dst': dst, 'edge_type_5': edge_type_5, 'L0_gnn_edge_type_weights': _L0_gnn_in['edge_type_weights'], 'L0_gnn_wq': _L0_gnn_in['wq'], 'L0_gnn_bq': _L0_gnn_in['bq'], 'L0_gnn_wk': _L0_gnn_in['wk'], 'L0_gnn_bk': _L0_gnn_in['bk'], 'L0_gnn_wv': _L0_gnn_in['wv'], 'L0_gnn_bv': _L0_gnn_in['bv'], 'L0_gnn_wiq': _L0_gnn_in['wiq'], 'L0_gnn_biq': _L0_gnn_in['biq'], 'L0_gnn_wik': _L0_gnn_in['wik'], 'L0_gnn_bik': _L0_gnn_in['bik'], 'L0_gnn_wiv': _L0_gnn_in['wiv'], 'L0_gnn_biv': _L0_gnn_in['biv'], 'L0_gnn_wo': _L0_gnn_in['wo'], 'L0_gnn_bo': _L0_gnn_in['bo'], 'L0_ffn_ternary_weight': _L0_ffn_in['ternary_weight'], 'L0_ffn_bias': _L0_ffn_in['bias'], 'L0_ffn_act_scale': _L0_ffn_in['act_scale']}

def reference(x, src, dst, edge_type_5, L0_gnn_edge_type_weights, L0_gnn_wq, L0_gnn_bq, L0_gnn_wk, L0_gnn_bk, L0_gnn_wv, L0_gnn_bv, L0_gnn_wiq, L0_gnn_biq, L0_gnn_wik, L0_gnn_bik, L0_gnn_wiv, L0_gnn_biv, L0_gnn_wo, L0_gnn_bo, L0_ffn_ternary_weight, L0_ffn_bias, L0_ffn_act_scale):
    import jax
    import jax.numpy as jnp

    def _L0_gnn_ref(x, edge_index, edge_type, edge_type_weights, wq, bq, wk, bk, wv, bv, wiq, biq, wik, bik, wiv, biv, wo, bo):
        import jax, jax.numpy as jnp
        import numpy as np
        N = 96
        E = 3072
        IN_F = 1024
        OUT_F = 1024
        H = 16
        D = OUT_F // H
        NUM_ETYPES = 4

        def _build_mask(edge_index, edge_type, edge_type_weights, dtype):
            src, dst = (edge_index[0], edge_index[1])
            w = jax.nn.softplus(edge_type_weights)
            mask = jnp.full((N, N), -jnp.inf, dtype=dtype)
            mask = mask.at[src, dst].set(w[edge_type - 1])
            diag = jnp.diagonal(mask)
            idx = jnp.arange(N)
            mask = mask.at[idx, idx].set(jnp.where(jnp.isneginf(diag), w[3], diag))
            return mask
        q = x @ wq.T + bq
        k = x @ wk.T + bk
        v = x @ wv.T + bv
        q2 = (q @ wiq.T + biq).reshape(N, H, D).transpose(1, 0, 2)
        k2 = (k @ wik.T + bik).reshape(N, H, D).transpose(1, 0, 2)
        v2 = (v @ wiv.T + biv).reshape(N, H, D).transpose(1, 0, 2)
        mask = _build_mask(edge_index, edge_type, edge_type_weights, x.dtype)
        scale = 1.0 / np.sqrt(D).astype(np.float32)
        scores = jnp.einsum('hnd,hmd->hnm', q2, k2) * scale + mask[None]
        attn = jax.nn.softmax(scores, axis=-1)
        out = jnp.einsum('hnm,hmd->hnd', attn, v2)
        out = out.transpose(1, 0, 2).reshape(N, OUT_F)
        return out @ wo.T + bo

    def _L0_ffn_ref(x, ternary_weight, bias, act_scale):
        import jax, jax.numpy as jnp
        import numpy as np
        B, S, D_IN, D_OUT = (16, 128, 1024, 1024)
        ACT_BITS = 8
        QB = float(2 ** (ACT_BITS - 1) - 1)
        scale = jnp.maximum(act_scale, 1e-05)
        x_int = jnp.clip(jnp.round(x / scale), -QB, QB)
        x_dq = jnp.nan_to_num(x_int * scale, nan=0.0, posinf=10000.0, neginf=-10000.0)
        w = ternary_weight.astype(jnp.float32) - 1.0
        return jnp.einsum('bsi,oi->bso', x_dq, w) + bias
    edge_index = jnp.stack([src, dst])
    x = x + _L0_gnn_ref(_layernorm(x, axis=-1), edge_index, edge_type_5, L0_gnn_edge_type_weights, L0_gnn_wq, L0_gnn_bq, L0_gnn_wk, L0_gnn_bk, L0_gnn_wv, L0_gnn_bv, L0_gnn_wiq, L0_gnn_biq, L0_gnn_wik, L0_gnn_bik, L0_gnn_wiv, L0_gnn_biv, L0_gnn_wo, L0_gnn_bo)
    x = x + _L0_ffn_ref(_layernorm(x, axis=-1)[None], L0_ffn_ternary_weight, L0_ffn_bias, L0_ffn_act_scale)[0]
    return x

_drawn_inputs = setup_inputs


def setup_inputs(seed=0):
    import zlib

    import numpy as np

    out = dict(_drawn_inputs(seed))
    spreads = {}
    factors = {'L0_gnn_edge_type_weights': 15.208,
     'L0_gnn_wq': 4.145,
     'L0_gnn_bq': 8.0,
     'L0_gnn_wk': 4.135,
     'L0_gnn_bk': 64.0,
     'L0_gnn_bv': 4.247,
     'L0_gnn_wiq': 4.161,
     'L0_gnn_biq': 8.0,
     'L0_gnn_wik': 4.166,
     'L0_gnn_bik': 64.0,
     'L0_gnn_biv': 3.364}
    for name, (base, spread) in spreads.items():
        noise = np.random.default_rng([zlib.crc32(name.encode()), seed]).standard_normal(out[name].shape)
        drawn = base * np.exp(spread * noise) if base else spread * noise
        out[name] = jnp.asarray(drawn.astype(out[name].dtype))
    for name, factor in factors.items():
        out[name] = (out[name] * factor).astype(out[name].dtype)
    return out
```

```python
from contextlib import ExitStack

import concourse.bass as bass
from concourse import mybir

ALU = mybir.AluOpType
ACT = mybir.ActivationFunctionType
AX = mybir.AxisListType
F32 = mybir.dt.float32
BF16 = mybir.dt.bfloat16
I32 = mybir.dt.int32
U32 = mybir.dt.uint32

P = 128
N = 96
F = 1024
T = F // P
H = 16
D = F // H
E = 3072
EG = 64
NG = E // EG
HG = 4
LN_EPS = 1e-5
SCALE = 1.0 / 8.0
QB = 127.0
ROUND = 1.5 * 2.0 ** 23

NO_EDGE = -3.0e38

BIAS = 0
ETW = 8 * T
ACTS = ETW + 4
SMALL = ACTS + 1
IDENT = 0
IOTA = IDENT + P
RANK = IOTA + N
DIAG = RANK + 1
CONST = DIAG + N


def gnn_ffn(nc, x_t, small, const, edges, w_proj, w_ternary, out):
    ctx = ExitStack()
    with ctx:
        def sb(name, shape, dt=F32):
            return ctx.enter_context(nc.sbuf_tensor(name, shape, dt))

        def bank(name):
            return ctx.enter_context(nc.psum_tensor(name, [P, 512], F32))

        def sem(name):
            return ctx.enter_context(nc.semaphore(name))

        slot_a = sb("slot_a", [P, T, F])
        slot_b = sb("slot_b", [P, T, F])
        slot_c = sb("slot_c", [P, T, F])
        slot_d = sb("slot_d", [P, T, F])

        small_sb = sb("small_sb", [P, SMALL])
        const_sb = sb("const_sb", [P, CONST])
        edges_sb = sb("edges_sb", [EG, 3 * NG], I32)
        ones = sb("ones", [P, P])
        eps = sb("eps", [P, 1])
        x = sb("x", [P, T, N])
        xc = sb("xc", [P, T, N])
        sq = sb("sq", [P, T, N])
        tsum = sb("tsum", [P, N])
        ssum = sb("ssum", [P, N])
        std = sb("std", [P, N])
        rstd = sb("rstd", [P, N])
        xn = sb("xn", [P, T, N])
        qkv = sb("qkv", [P, 3 * T, N])
        q2 = sb("q2", [P, T, N])
        k2 = sb("k2", [P, T, N])
        v2t = sb("v2t", [P, T, N])
        v2 = sb("v2", [N, F])
        att = sb("att", [N, H, N])
        att_t = sb("att_t", [N, H, N])
        outt = sb("outt", [P, T, N])
        x1 = sb("x1", [P, T, N])
        x1b = sb("x1b", [P, T, N])
        xi = sb("xi", [P, T, N], BF16)
        xgood = sb("xgood", [P, T, N], BF16)
        fin = sb("fin", [P, T, N])
        smax = sb("smax", [N, H])
        ssm = sb("ssm", [N, H])
        rsm = sb("rsm", [N, H])
        edges_f = sb("edges_f", [EG, 3 * NG])
        typ3 = sb("typ3", [EG, NG])
        lvl = sb("lvl", [EG, NG])
        vote_w = sb("vote_w", [EG, NG])
        edge_tab = sb("edge_tab", [EG, NG, 3])
        edge_now = sb("edge_now", [EG, 2, 2, 3])
        src_hot = sb("src_hot", [EG, 2, 2, N], BF16)
        dst_hot = sb("dst_hot", [EG, 2, 2, N], BF16)
        blank = sb("blank", [N, 2, N])
        winner = sb("winner", [N, N])
        code = sb("code", [N, N], U32)
        sixth = sb("sixth", [N, N])
        typ = sb("typ", [N, N])
        is_typ = sb("is_typ", [N, 4, N], U32)
        mask = sb("mask", [N, N])
        wsp = sb("wsp", [N, 5, 4])
        scl = sb("scl", [P, 6])

        proj_ps = [bank("proj_ps0"), bank("proj_ps1")]
        mid = [bank(f"mid{i}") for i in range(4)]
        end = [bank("end0"), bank("end1")]
        vote_ps = mid[0:2]
        score_ps = mid
        stat_ps = end[0]

        s_x = sem("s_x")
        s_small = sem("s_small")
        s_const = sem("s_const")
        s_edges = sem("s_edges")
        landed_a = [sem(f"landed_a{j}") for j in range(T)]
        landed_b = [sem(f"landed_b{j}") for j in range(T)]
        landed_c = [sem(f"landed_c{j}") for j in range(T)]
        landed_d = [sem(f"landed_d{j}") for j in range(T)]
        proj_done = sem("proj_done")
        proj_free = sem("proj_free")
        edge_step = sem("edge_step")
        hot_ready = sem("hot_ready")
        votes_done = sem("votes_done")
        votes_free = sem("votes_free")
        pool_step = sem("pool_step")
        dve_step = sem("dve_step")
        act_step = sem("act_step")
        s_tsum = sem("s_tsum")
        s_mean = sem("s_mean")
        s_xc = sem("s_xc")
        s_sq = sem("s_sq")
        s_ssum = sem("s_ssum")
        s_var = sem("s_var")
        s_std = sem("s_std")
        s_xn = sem("s_xn")
        s_etw = sem("s_etw")
        s_scores = sem("s_scores")
        s_shift = sem("s_shift")
        s_exp = sem("s_exp")
        s_att = sem("s_att")
        s_attT = sem("s_attT")
        s_attT_sb = sem("s_attT_sb")
        s_v2 = sem("s_v2")
        s_v2_sb = sem("s_v2_sb")
        s_pv = sem("s_pv")
        s_pv_sb = sem("s_pv_sb")
        s_x1 = sem("s_x1")
        s_tern = sem("s_tern")
        s_xi = sem("s_xi")
        s_ffn = sem("s_ffn")
        s_fin = sem("s_fin")
        s_out = sem("s_out")

        ident = const_sb[:, IDENT:IDENT + P]
        iota = const_sb[0:EG, IOTA:IOTA + N]
        w_bf = slot_c[:, 0:T // 2, :].rearrange("p a b -> p (a b)").bitcast(BF16).rearrange(
            "p (o c) -> p o c", o=T)

        def head(h):
            par, u = h % 2, h // 2
            g = 2 * par + u // HG
            return par, u, g, u % HG, g * HG + u % HG

        block = ctx.enter_context(nc.Block())

        @block.sync
        def _(sp):
            for j in range(T):
                sp.dma_start(slot_a[:, j, :], w_proj[0, j]).then_inc(landed_a[j], 16)
            with sp.Fori(1, 3) as s:
                for j in range(T):
                    sp.wait_ge(proj_done, s * T + (j + 1 - T))
                    sp.dma_start(slot_a[:, j, :], w_proj[bass.ds(s, 1), j].rearrange("a p c -> p (a c)")).then_inc(landed_a[j], 16)
            for j in range(T):
                sp.dma_start(slot_b[:, j, :], w_proj[3, j]).then_inc(landed_b[j], 16)
            for j in range(T):
                sp.dma_start(slot_c[:, j, :], w_proj[4, j]).then_inc(landed_c[j], 16)
            for j in range(T):
                sp.dma_start(slot_d[:, j, :], w_proj[5, j]).then_inc(landed_d[j], 16)
            for j in range(T):
                sp.wait_ge(proj_done, 3 * T + j + 1)
                sp.dma_start(slot_b[:, j, :], w_proj[6, j]).then_inc(landed_b[j], 16)
            for j in range(T):
                sp.wait_ge(proj_done, 2 * T + j + 1)
                sp.dma_start(slot_a[:, j, :].bitcast(I32), w_ternary[j]).then_inc(landed_a[j], 16)
            for o in range(T):
                sp.wait_ge(s_fin, o + 1)
                sp.dma_start(out[:, o, :], fin[:, o, :]).then_inc(s_out, 16)
            sp.wait_ge(s_out, 16 * T)

        @block.gpsimd
        def _(pool):
            n = 0
            pool.wait_ge(s_edges, 16)
            nc.gpsimd.tensor_copy(edges_f[:], edges_sb[:]).then_inc(pool_step, 1)
            etype = edges_f[:, 2 * NG:3 * NG]
            pool.wait_ge(pool_step, 1)
            nc.gpsimd.tensor_scalar(typ3[:], etype, 4.0, None, ALU.is_equal).then_inc(pool_step, 1)
            nc.gpsimd.tensor_scalar(lvl[:], etype, 0.0, 2.5, ALU.is_equal, ALU.mult).then_inc(pool_step, 1)
            pool.wait_ge(pool_step, 3)
            nc.gpsimd.tensor_tensor(lvl[:], lvl[:], typ3[:], ALU.add).then_inc(pool_step, 1)
            pool.wait_ge(pool_step, 4)
            nc.gpsimd.tensor_scalar(typ3[:], typ3[:], -0.5, 0.5, ALU.mult, ALU.add).then_inc(pool_step, 1)
            nc.gpsimd.tensor_scalar(vote_w[:], etype, 0.5, 0.0, ALU.mult, ALU.add).then_inc(pool_step, 1)
            pool.wait_ge(pool_step, 6)
            nc.gpsimd.tensor_tensor(lvl[:], lvl[:], typ3[:], ALU.add).then_inc(pool_step, 1)
            pool.wait_ge(pool_step, 7)
            nc.gpsimd.tensor_tensor(lvl[:], lvl[:], vote_w[:], ALU.add).then_inc(pool_step, 1)
            pool.wait_ge(pool_step, 8)
            pool.wait_ge(s_const, 16)
            nc.gpsimd.tensor_scalar(vote_w[:], lvl[:], const_sb[0:EG, RANK:RANK + 1], 1.0, ALU.mult, ALU.mult).then_inc(pool_step, 1)
            pool.wait_ge(pool_step, 9)
            nc.gpsimd.tensor_copy(edge_tab[:, :, 0], edges_f[:, 0:NG]).then_inc(pool_step, 1)
            nc.gpsimd.tensor_copy(edge_tab[:, :, 1], vote_w[:]).then_inc(pool_step, 1)
            nc.gpsimd.tensor_copy(edge_tab[:, :, 2], edges_f[:, NG:2 * NG]).then_inc(pool_step, 1)
            pool.wait_ge(pool_step, 12)
            with pool.Fori(0, 3) as s:
                for j in range(T):
                    pool.wait_ge(votes_done, s * T + (j + 1))
                    nc.gpsimd.tensor_copy(edge_now[:, j % 2, :, :], edge_tab[:, bass.ds(s * (2 * T) + 2 * j, 2), :]).then_inc(edge_step, 1)
                    pool.wait_ge(edge_step, s * T + (j + 1))
                    pool.nop(nofuse=True)
                    for g in range(2):
                        nc.gpsimd.tensor_scalar(src_hot[:, j % 2, g, :], iota, edge_now[:, j % 2, g, 0:1],
                                                edge_now[:, j % 2, g, 1:2], ALU.is_equal, ALU.mult)
                        last = nc.gpsimd.tensor_scalar(dst_hot[:, j % 2, g, :], iota,
                                                       edge_now[:, j % 2, g, 2:3], 1.0,
                                                       ALU.is_equal, ALU.mult)
                    last.then_inc(hot_ready, 1)
            pool.wait_ge(s_x1, T)
            nc.gpsimd.tensor_tensor(x1b[:], x1[:], small_sb[:, BIAS + 7 * T:BIAS + 8 * T].unsqueeze(2).to_broadcast([P, T, N]),
                                    ALU.add).then_inc(pool_step, 1)

        @block.scalar
        def _(act):
            act.dma_start(x[:], x_t).then_inc(s_x, 16)
            act.dma_start(edges_sb[:], edges).then_inc(s_edges, 16)
            act.dma_start(const_sb[:], const).then_inc(s_const, 16)
            act.dma_start(small_sb[:], small).then_inc(s_small, 16)

            def layernorm(n):
                act.wait_ge(s_xc, n + 1)
                nc.scalar.activation(sq[:], xc[:], ACT.Square).then_inc(s_sq, 1)
                act.wait_ge(s_var, n + 1)
                nc.scalar.activation(std[:], stat_ps[:, N:2 * N], ACT.Sqrt, bias=eps[:, 0:1]).then_inc(s_std, 1)

            layernorm(0)
            act.sem_inc(proj_free, 2)
            act.wait_ge(s_small, 16)
            act.wait_ge(s_etw, 1)
            nc.scalar.activation(wsp[:, 1, :], wsp[:, 0, :], ACT.Exp, scale=-1.0).then_inc(act_step, 1)
            act.wait_ge(act_step, 1)
            nc.scalar.activation(wsp[:, 2, :], wsp[:, 1, :], ACT.Ln, bias=1.0).then_inc(act_step, 1)
            with act.Fori(0, 3) as s:
                for j in range(T):
                    act.wait_ge(proj_done, s * T + (j + 1))
                    nc.scalar.activation(qkv[:, bass.ds(s * T + j, 1), :].rearrange("p a n -> p (a n)"),
                                         proj_ps[j % 2][:, 0:N], ACT.Identity,
                                         bias=small_sb[:, bass.ds(s * T + (BIAS + j), 1)]).then_inc(proj_free, 1)

            def evacuate(s, dst):
                for j in range(T):
                    act.wait_ge(proj_done, s * T + j + 1)
                    nc.scalar.activation(dst[:, j, :], proj_ps[j % 2][:, 0:N], ACT.Identity,
                                         bias=small_sb[:, BIAS + s * T + j:BIAS + s * T + j + 1]).then_inc(proj_free, 1)

            evacuate(3, q2)
            evacuate(4, k2)
            for g in range(4):
                act.wait_ge(s_shift, g + 1)
                nc.scalar.activation(att[:, g * HG:(g + 1) * HG, :], att[:, g * HG:(g + 1) * HG, :],
                                     ACT.Exp).then_inc(s_exp, 1)
            evacuate(5, v2t)
            layernorm(1)

        @block.tensor
        def _(pe):
            def tile(s, j, weights, moving, k0=0):
                for k in range(T):
                    mm = nc.tensor.matmul(proj_ps[j % 2][:, 0:N], weights[:, j, k * P:(k + 1) * P],
                                          moving[:, k0 + k, :], start=(k == 0), stop=(k == T - 1))
                mm.then_inc(proj_done, 1)

            def node_sums(n):
                pe.wait_ge(s_tsum, n + 1)
                nc.tensor.matmul(stat_ps[:, 0:N], ones[:], tsum[:], start=True, stop=True).then_inc(s_mean, 1)
                pe.wait_ge(s_ssum, n + 1)
                nc.tensor.matmul(stat_ps[:, N:2 * N], ones[:], ssum[:], start=True, stop=True).then_inc(s_var, 1)

            node_sums(0)
            pe.sem_inc(votes_done, 2)
            pe.wait_ge(s_xn, 1)
            with pe.Fori(0, 3) as s:
                for j in range(T):
                    pe.wait_ge(landed_a[j], s * 16 + 16)
                    pe.wait_ge(proj_free, s * T + (j + 1))
                    tile(s, j, slot_a, xn)
                    pe.wait_ge(hot_ready, s * T + (j + 1))
                    pe.wait_ge(votes_free, s * T + (j + 1))
                    for g in range(2):
                        mm = nc.tensor.matmul(vote_ps[j % 2][0:N, g * N:(g + 1) * N], src_hot[:, j % 2, g, :],
                                              dst_hot[:, j % 2, g, :], start=True, stop=True)
                    mm.then_inc(votes_done, 1)

            def stage(s, weights, landed, times, moving, k0):
                for j in range(T):
                    pe.wait_ge(landed[j], 16 * times)
                    pe.wait_ge(proj_free, s * T + j + 1)
                    tile(s, j, weights, moving, k0)

            pe.wait_ge(proj_free, 3 * T + 2)
            stage(3, slot_b, landed_b, 1, qkv, 0)
            stage(4, slot_c, landed_c, 1, qkv, T)
            pe.wait_ge(proj_free, 5 * T + 2)
            for h in range(H):
                par, u, g, i, _ = head(h)
                if h == 0:
                    pe.wait_ge(votes_free, 3 * T + 2)
                rows = slice(D * par, D * par + D)
                mm = nc.tensor.matmul(score_ps[g][0:N, i * N:(i + 1) * N], q2[rows, u, :], k2[rows, u, :],
                                      start=True, stop=True)
            mm.then_inc(s_scores, 1)
            stage(5, slot_d, landed_d, 1, qkv, 2 * T)
            pe.wait_ge(proj_free, 6 * T + 2)
            for u in range(T):
                mm = nc.tensor.transpose(end[u // 4][0:N, (u % 4) * P:(u % 4 + 1) * P], v2t[:, u, :], ident)
                if u % 4 == 3:
                    mm.then_inc(s_v2, 1)
            for g in range(4):
                pe.wait_ge(s_att, g + 1)
                for i in range(HG):
                    mm = nc.tensor.transpose(score_ps[g][0:N, i * N:(i + 1) * N], att[:, g * HG + i, :],
                                             ident[0:N, 0:N])
                mm.then_inc(s_attT, 1)
            pe.wait_ge(s_attT_sb, 4)
            pe.wait_ge(s_v2_sb, 2)
            for h in range(H):
                par, u, g, i, a = head(h)
                mm = nc.tensor.matmul(end[u // 4][D * par:D * par + D, (u % 4) * N:(u % 4 + 1) * N],
                                      v2[:, h * D:(h + 1) * D], att_t[:, a, :], start=True, stop=True)
            mm.then_inc(s_pv, 1)
            pe.wait_ge(s_pv_sb, 2)
            stage(6, slot_b, landed_b, 2, outt, 0)
            node_sums(1)
            pe.wait_ge(s_xi, 1)
            for o in range(T):
                pe.wait_ge(s_tern, o + 1)
                if o >= 4:
                    pe.wait_ge(s_fin, o - 3)
                if o < 4:
                    bk = mid[o]
                else:
                    bk = mid[o % 4]
                for k in range(T):
                    mm = nc.tensor.matmul(bk[:, 0:N], w_bf[:, o, k * P:(k + 1) * P], xi[:, k, :],
                                          start=(k == 0), stop=(k == T - 1))
                mm.then_inc(s_ffn, 1)

        @block.vector
        def _(dve):
            steps = [0]

            def step(ins):
                steps[0] += 1
                ins.then_inc(dve_step, 1)
                dve.wait_ge(dve_step, steps[0])

            def bcast(a):
                return a.unsqueeze(1).to_broadcast([P, T, N])

            def layernorm_stats(n, src):
                nc.vector.tensor_reduce(tsum[:], src[:].rearrange("p t n -> p n t"), AX.X, ALU.add).then_inc(s_tsum, 1)
                dve.wait_ge(s_mean, n + 1)
                nc.vector.tensor_tensor(xc[:], src[:], bcast(stat_ps[:, 0:N]), ALU.subtract).then_inc(s_xc, 1)
                dve.wait_ge(s_sq, n + 1)
                nc.vector.tensor_reduce(ssum[:], sq[:].rearrange("p t n -> p n t"), AX.X, ALU.add).then_inc(s_ssum, 1)
                dve.wait_ge(s_std, n + 1)
                step(nc.vector.reciprocal(rstd[:], std[:]))

            nc.vector.memset(eps[:], LN_EPS)
            step(nc.vector.memset(ones[:], 1.0 / F))
            dve.wait_ge(s_x, 16)
            layernorm_stats(0, x)
            nc.vector.tensor_tensor(xn[:], xc[:], bcast(rstd[:]), ALU.mult).then_inc(s_xn, 1)

            dve.wait_ge(s_small, 16)
            step(nc.vector.tensor_scalar(wsp[:, 3, :], small_sb[0:N, ETW:ETW + 4], 0.0, None, ALU.max))
            nc.vector.scalar_tensor_tensor(out=wsp[:, 0, :], in0=wsp[:, 3, :], scalar=2.0,
                                           in1=small_sb[0:N, ETW:ETW + 4], op0=ALU.mult,
                                           op1=ALU.subtract).then_inc(s_etw, 1)
            step(nc.vector.tensor_scalar(scl[:, 0:1], small_sb[:, ACTS:ACTS + 1], 1e-5, None, ALU.max))
            step(nc.vector.reciprocal(scl[:, 1:2], scl[:, 0:1]))

            dve.wait_ge(s_const, 16)
            step(nc.vector.tensor_copy(winner[:], const_sb[0:N, DIAG:DIAG + N]))
            dve.sem_inc(votes_free, 2)
            base = steps[0]
            with dve.Fori(0, 3) as s:
                for j in range(T):
                    dve.wait_ge(votes_done, s * T + (j + 3))
                    nc.vector.tensor_scalar(blank[:], vote_ps[j % 2][0:N, 0:2 * N].rearrange(
                        "p (g n) -> p g n", g=2), 0.0, None, ALU.is_equal).then_inc(dve_step, 1)
                    for g in range(2):
                        at = base + 4 * j + 2 * g + 1
                        dve.wait_ge(dve_step, s * (4 * T) + at)
                        nc.vector.tensor_tensor(winner[:], winner[:], blank[:, g, :], ALU.mult).then_inc(dve_step, 1)
                        dve.wait_ge(dve_step, s * (4 * T) + (at + 1))
                        last = nc.vector.tensor_tensor(winner[:], winner[:], vote_ps[j % 2][0:N, g * N:(g + 1) * N], ALU.add)
                        if g == 0:
                            last.then_inc(dve_step, 1)
                    last.then_inc(votes_free, 1)
                    dve.wait_ge(votes_free, s * T + (j + 3))
            steps[0] += 4 * T * 3
            step(nc.vector.tensor_scalar(code[:], winner[:].bitcast(U32), 22, None, ALU.logical_shift_right))
            step(nc.vector.tensor_scalar(sixth[:], code[:], 63.5, 1.0 / 6.0, ALU.subtract, ALU.mult))
            step(nc.vector.tensor_scalar(sixth[:], sixth[:], ROUND, ROUND, ALU.add, ALU.subtract))
            step(nc.vector.scalar_tensor_tensor(out=typ[:], in0=sixth[:], scalar=-6.0, in1=code[:],
                                                op0=ALU.mult, op1=ALU.add))
            nc.vector.memset(mask[:], NO_EDGE)
            dve.wait_ge(act_step, 2)
            step(nc.vector.tensor_tensor(wsp[:, 4, :], wsp[:, 2, :], wsp[:, 3, :], ALU.add))
            for t in range(4):
                last = nc.vector.tensor_scalar(is_typ[:, t, :], typ[:], 62.0 + t, None, ALU.is_equal)
            step(last)
            for t in range(4):
                step(nc.vector.copy_predicated(mask[:], is_typ[:, t, :], wsp[:, 4, t:t + 1].to_broadcast([N, N])))

            dve.wait_ge(s_scores, 1)
            for g in range(4):
                heads = slice(g * HG, (g + 1) * HG)
                a = att[:, heads, :]
                step(nc.vector.scalar_tensor_tensor(
                    out=a, in0=score_ps[g][0:N, 0:HG * N].rearrange("p (h n) -> p h n", h=HG), scalar=SCALE,
                    in1=mask[:].unsqueeze(1).to_broadcast([N, HG, N]), op0=ALU.mult, op1=ALU.add))
                step(nc.vector.tensor_reduce(smax[:, heads], a, AX.X, ALU.max))
                nc.vector.tensor_tensor(a, a, smax[:, heads].unsqueeze(2).to_broadcast([N, HG, N]),
                                        ALU.subtract).then_inc(s_shift, 1)
            for g in range(4):
                heads = slice(g * HG, (g + 1) * HG)
                a = att[:, heads, :]
                dve.wait_ge(s_exp, g + 1)
                step(nc.vector.tensor_reduce(ssm[:, heads], a, AX.X, ALU.add))
                step(nc.vector.reciprocal(rsm[:, heads], ssm[:, heads]))
                nc.vector.tensor_tensor(a, a, rsm[:, heads].unsqueeze(2).to_broadcast([N, HG, N]),
                                        ALU.mult).then_inc(s_att, 1)
            for b in range(2):
                dve.wait_ge(s_v2, b + 1)
                nc.vector.tensor_copy(v2[:, b * 512:(b + 1) * 512], end[b][0:N, :]).then_inc(s_v2_sb, 1)
            for g in range(4):
                dve.wait_ge(s_attT, g + 1)
                nc.vector.tensor_copy(att_t[:, g * HG:(g + 1) * HG, :],
                                      score_ps[g][0:N, 0:HG * N].rearrange("p (h n) -> p h n", h=HG)).then_inc(s_attT_sb, 1)
            dve.wait_ge(s_pv, 1)
            for b in range(2):
                nc.vector.tensor_copy(outt[:, b * 4:(b + 1) * 4, :],
                                      end[b][:, 0:4 * N].rearrange("p (u n) -> p u n", u=4)).then_inc(s_pv_sb, 1)
            for j in range(T):
                dve.wait_ge(proj_done, 6 * T + j + 1)
                nc.vector.scalar_tensor_tensor(out=x1[:, j, :], in0=proj_ps[j % 2][:, 0:N],
                                               scalar=small_sb[:, BIAS + 6 * T + j:BIAS + 6 * T + j + 1],
                                               in1=x[:, j, :], op0=ALU.add, op1=ALU.add).then_inc(proj_free, 1)
                dve.wait_ge(proj_free, 6 * T + j + 3)
            dve.sem_inc(s_x1, T)
            layernorm_stats(1, x1)
            step(nc.vector.tensor_scalar(rstd[:], rstd[:], scl[:, 1:2], None, ALU.mult))
            step(nc.vector.tensor_tensor(xc[:], xc[:], bcast(rstd[:]), ALU.mult))
            nc.vector.tensor_tensor(xgood[:], xc[:], xc[:], ALU.is_equal)
            step(nc.vector.tensor_scalar(sq[:], xc[:], QB, -QB, ALU.min, ALU.max))
            step(nc.vector.tensor_scalar(xi[:], sq[:], ROUND, ROUND, ALU.add, ALU.subtract))
            nc.vector.tensor_tensor(xi[:], xi[:], xgood[:], ALU.mult).then_inc(s_xi, 1)
            for j in range(T):
                dve.wait_ge(landed_a[j], 64)
                nc.vector.tensor_scalar(w_bf[:, j, :], slot_a[:, j, :].bitcast(I32), -1.0, None, ALU.add).then_inc(s_tern, 1)
            for o in range(T):
                dve.wait_ge(s_ffn, o + 1)
                if o == 0:
                    dve.wait_ge(pool_step, 13)
                nc.vector.scalar_tensor_tensor(out=fin[:, o, :], in0=mid[o % 4][:, 0:N], scalar=scl[:, 0:1],
                                               in1=x1b[:, o, :], op0=ALU.mult, op1=ALU.add).then_inc(s_fin, 1)


def kernel(x, src, dst, edge_type_5, L0_gnn_edge_type_weights, L0_gnn_wq, L0_gnn_bq, L0_gnn_wk, L0_gnn_bk,
           L0_gnn_wv, L0_gnn_bv, L0_gnn_wiq, L0_gnn_biq, L0_gnn_wik, L0_gnn_bik, L0_gnn_wiv, L0_gnn_biv,
           L0_gnn_wo, L0_gnn_bo, L0_ffn_ternary_weight, L0_ffn_bias, L0_ffn_act_scale):
    import numpy as np
    import concourse.bacc as bacc
    from concourse.bass_utils import run_bass_kernel_spmd

    def chunks(w):
        return np.asarray(w).reshape(T, P, T, P).transpose(0, 3, 2, 1).reshape(T, P, F)

    small = np.empty((P, SMALL), np.float32)
    for i, b in enumerate((L0_gnn_bq, L0_gnn_bk, L0_gnn_bv, L0_gnn_biq, L0_gnn_bik, L0_gnn_biv, L0_gnn_bo,
                           L0_ffn_bias)):
        small[:, BIAS + i * T:BIAS + (i + 1) * T] = np.asarray(b).reshape(T, P).T
    small[:, ETW:ETW + 4] = np.asarray(L0_gnn_edge_type_weights)[None, :]
    small[:, ACTS] = np.asarray(L0_ffn_act_scale)
    const = np.zeros((P, CONST), np.float32)
    const[:, IDENT:IDENT + P] = np.eye(P)
    const[:, IOTA:IOTA + N] = np.arange(N)[None, :]
    const[:, RANK] = 2.0 ** (3.0 * (np.arange(P) % EG) - 96.0)
    const[:N, DIAG:DIAG + N] = np.eye(N) * 3.0 * 2.0 ** -96
    arrays = {
        "in_x_t": np.ascontiguousarray(np.asarray(x).reshape(N, T, P).transpose(2, 1, 0)),
        "in_small": small,
        "in_const": const,
        "in_edges": np.ascontiguousarray(np.concatenate(
            [np.asarray(a).reshape(NG, EG).T for a in (src, dst, edge_type_5)], axis=1)),
        "in_w_proj": np.stack([chunks(w) for w in (L0_gnn_wq, L0_gnn_wk, L0_gnn_wv, L0_gnn_wiq, L0_gnn_wik,
                                                   L0_gnn_wiv, L0_gnn_wo)]),
        "in_w_ternary": np.ascontiguousarray(chunks(L0_ffn_ternary_weight)),
    }
    nc = bacc.Bacc("TRN2", target_bir_lowering=False, num_devices=1)
    aps = [nc.dram_tensor(name, a.shape, mybir.dt.from_np(a.dtype), kind="ExternalInput").ap()
           for name, a in arrays.items()]
    out = nc.dram_tensor("out", (P, T, N), F32, kind="ExternalOutput").ap()
    gnn_ffn(nc, *aps, out)
    r = run_bass_kernel_spmd(nc, [arrays], core_ids=[0])
    return r.results[0]["out"].reshape(P, T, N).transpose(2, 1, 0).reshape(N, F)
```

```python
from contextlib import ExitStack

import concourse.bass as bass
from concourse import mybir

ALU = mybir.AluOpType
ACT = mybir.ActivationFunctionType
AX = mybir.AxisListType
F32 = mybir.dt.float32
F32R = mybir.dt.float32r
BF16 = mybir.dt.bfloat16
I32 = mybir.dt.int32
U32 = mybir.dt.uint32

P = 128
N = 96
F = 1024
T = F // P
W = 512
H = 16
D = F // H
HG = 4
E = 3072
EG = 64
EC = E // P
C = 8
SC = C // 2
M = 2 * C
R = 4
RL = 6
AHEAD = 3
VC = 6
LN_EPS = 1e-5
SCALE = 1.0 / 8.0
QB = 127.0
ROUND = 1.5 * 2.0 ** 23
BIG = 3.0e38
NO_EDGE = -3.0e38
ORDER = (0, 2, 1, 3)

BY_POOL = [1, 3, 5, 8, 10, 12, 14]
BY_DVE = [j for j in range(M) if j not in BY_POOL]
LAST_POOL = [3, 5, 7, 9, 10, 12, 17, 19, 21]
LAST_DVE = [j for j in range(AHEAD, M + C) if j not in LAST_POOL]
TURN_AFTER = (5, 8, 13, 16)
NAT_AFTER = (7, 12, 16, 20)

BIAS = 0
ETW = 6 * T
ACTS = ETW + 4
SMALL = ACTS + 1
IDENT = 0
IOTA = IDENT + P
RANK = IOTA + N
DIAG = RANK + 1
CONST = DIAG + N


def lower_count(s, j):
    last = isinstance(s, int) and s == 2
    for by_pool, mine, in_last in ((True, BY_POOL, LAST_POOL), (False, BY_DVE, LAST_DVE)):
        if last and j in in_last:
            return by_pool, 2 * len(mine) + len([c for c in mine if c < AHEAD]) + in_last.index(j) + 1
        if not last and j % M in mine:
            return by_pool, s * len(mine) + (j // M * len(mine) + mine.index(j % M) + 1)


def ring(s, j):
    return j % (RL if isinstance(s, int) and s == 2 else R)


def gnn_ffn(nc, x_in, small, const, rows, edges, w_proj, w_ternary, out):
    ctx = ExitStack()
    with ctx:
        def sb(name, shape, dt=F32):
            return ctx.enter_context(nc.sbuf_tensor(name, shape, dt))

        def sem(name):
            return ctx.enter_context(nc.semaphore(name))

        slots = sb("slots", [P, M, F])
        w_hi = sb("w_hi", [P, RL, F], F32R)
        w_lo = sb("w_lo", [P, RL, F], F32R)
        w_bf = sb("w_bf", [P, C, F], BF16)

        small_sb = sb("small_sb", [P, SMALL])
        const_sb = sb("const_sb", [P, CONST])
        x = sb("x", [N, F])
        xn = sb("xn", [N, F])
        xn_hi = sb("xn_hi", [P, T, N], F32R)
        xn_lo = sb("xn_lo", [P, T, N], F32R)
        nat = sb("nat", [N, 2, W])
        full = sb("full", [P, 2, 4, N])
        act_hi = sb("act_hi", [P, T, N], F32R)
        act_lo = sb("act_lo", [P, T, N], F32R)
        qk2 = sb("qk2", [P, 2 * T, N])
        v2 = sb("v2", [N, F])
        att = sb("att", [N, H, N])
        att_t = sb("att_t", [N, H, N])
        out_hi, out_lo = xn_hi, xn_lo
        x1 = v2
        xi_t = sb("xi_t", [P, T, N], BF16)
        bo_sb = xn
        bias_row = sb("bias_row", [1, F])
        ones = sb("ones", [1, N])
        ln = sb("ln", [N, 32])
        warm = sb("warm", [P, 2])
        scl = sb("scl", [N, 6])
        smax = sb("smax", [N, H])
        ssm = sb("ssm", [N, H])
        rsm = sb("rsm", [N, H])
        edges_sb = sb("edges_sb", [P, 3 * EC], I32)
        edges_f = sb("edges_f", [P, 3 * EC])
        typ3 = sb("typ3", [P, EC])
        lvl = sb("lvl", [P, EC])
        vote_w = sb("vote_w", [P, EC])
        src_is = sb("src_is", [P, VC, N], BF16)
        src_hot = sb("src_hot", [P, VC, N], BF16)
        dst_hot = sb("dst_hot", [P, VC, N], BF16)
        new_votes = att[:].rearrange("p (g b a) n -> p g b a n", g=4, b=2)
        winner = sb("winner", [N, 2, 2, N])
        code = sb("code", [N, N], U32)
        sixth = sb("sixth", [N, N])
        typ = sb("typ", [N, N])
        is_typ = sb("is_typ", [N, 4, N], U32)
        mask = sb("mask", [N, N])
        wsp = sb("wsp", [N, 5, 4])

        proj_ps = ctx.enter_context(nc.psum_tensor("proj_ps", [P, 2, W], F32))
        turn_ps = ctx.enter_context(nc.psum_tensor("turn_ps", [P, 2, W], F32))
        mid = ctx.enter_context(nc.psum_tensor("mid", [P, 4, W], F32))

        s_x = sem("s_x")
        s_small = sem("s_small")
        s_const = sem("s_const")
        s_edges = sem("s_edges")
        s_bo = sem("s_bo")
        s_row = sem("s_row")
        landed = [sem(f"landed{j}") for j in range(M)]
        pool_step = sem("pool_step")
        dve_step = sem("dve_step")
        act_step = sem("act_step")
        s_var = sem("s_var")
        s_std = sem("s_std")
        s_xn = sem("s_xn")
        s_xn_turned = sem("s_xn_turned")
        s_xn_hi = sem("s_xn_hi")
        s_xn_lo = sem("s_xn_lo")
        w_hi_ready = sem("w_hi_ready")
        w_lo_dve = sem("w_lo_dve")
        w_lo_pool = sem("w_lo_pool")
        w_used = sem("w_used")
        nat_ready = sem("nat_ready")
        turned = sem("turned")
        full_ready = sem("full_ready")
        act_hi_ready = sem("act_hi_ready")
        act_ready = sem("act_ready")
        hot_is = sem("hot_is")
        hot_ready = sem("hot_ready")
        votes_done = sem("votes_done")
        votes_read = sem("votes_read")
        votes_kept = sem("votes_kept")
        s_etw = sem("s_etw")
        s_scores = sem("s_scores")
        s_max = sem("s_max")
        s_shift = sem("s_shift")
        s_exp = sem("s_exp")
        s_inv = sem("s_inv")
        s_att = sem("s_att")
        s_att_turned = sem("s_att_turned")
        s_att_t = sem("s_att_t")
        s_xb = sem("s_xb")
        s_x1 = sem("s_x1")
        s_bias = sem("s_bias")
        s_wbf = sem("s_wbf")
        s_xi = sem("s_xi")
        s_xi_turned = sem("s_xi_turned")
        s_xi_t = sem("s_xi_t")
        s_ffn = sem("s_ffn")
        s_fin = sem("s_fin")
        s_out = sem("s_out")

        ident = const_sb[:, IDENT:IDENT + P]
        iota = const_sb[:, IOTA:IOTA + N]

        def four(ap):
            return ap.rearrange("p (t n) -> p t n", t=4)

        block = ctx.enter_context(nc.Block())

        @block.sync
        def _(sp):
            sp.dma_start(x[:], x_in).then_inc(s_x, 16)
            for j in range(M):
                sp.dma_start(slots[:, j, :], w_proj[j // C, j % C]).then_inc(landed[j], 16)
            with sp.Fori(1, 3) as s:
                for j in range(M):
                    sp.wait_ge(w_used, s * M + (R + j + 1 - M))
                    sp.dma_start(slots[:, j, :], w_proj[bass.ds(s * 2 + j // C, 1), j % C].rearrange(
                        "a p c -> p (a c)")).then_inc(landed[j], 16)
            for j in range(C):
                sp.wait_ge(w_used, R + 2 * M + j + 1)
                sp.dma_start(slots[:, j, :], w_proj[6, j]).then_inc(landed[j], 16)
            sp.dma_start(bo_sb[:], rows[0:1, :].to_broadcast([N, F])).then_inc(s_bo, 16)
            sp.dma_start(bias_row[:], rows[1:2, :]).then_inc(s_row, 16)
            for j in range(C, M):
                sp.wait_ge(w_used, R + 2 * M + j + 1)
                sp.dma_start(slots[:, j, :].bitcast(I32), w_ternary[j - C]).then_inc(landed[j], 16)
            for h in range(2):
                sp.wait_ge(s_fin, h + 1)
                sp.dma_start(out[:, h * W:(h + 1) * W], x1[:, h * W:(h + 1) * W]).then_inc(s_out, 16)
            sp.wait_ge(s_out, 32)

        @block.gpsimd
        def _(pool):
            nc.gpsimd.memset(ones[:], 1.0).then_inc(pool_step, 1)
            pool.wait_ge(s_edges, 16)
            nc.gpsimd.tensor_copy(edges_f[:], edges_sb[:]).then_inc(pool_step, 1)
            etype = edges_f[:, 2 * EC:3 * EC]
            pool.wait_ge(pool_step, 2)
            nc.gpsimd.tensor_scalar(typ3[:], etype, 4.0, 0.5, ALU.is_equal, ALU.mult).then_inc(pool_step, 1)
            nc.gpsimd.tensor_scalar(lvl[:], etype, 0.0, 2.5, ALU.is_equal, ALU.mult).then_inc(pool_step, 1)
            nc.gpsimd.tensor_scalar(vote_w[:], etype, 0.5, 0.5, ALU.mult, ALU.add).then_inc(pool_step, 1)
            pool.wait_ge(pool_step, 5)
            nc.gpsimd.tensor_tensor(lvl[:], lvl[:], typ3[:], ALU.add).then_inc(pool_step, 1)
            pool.wait_ge(pool_step, 6)
            nc.gpsimd.tensor_tensor(lvl[:], lvl[:], vote_w[:], ALU.add).then_inc(pool_step, 1)
            pool.wait_ge(pool_step, 7)
            pool.wait_ge(s_const, 16)
            nc.gpsimd.tensor_scalar(vote_w[:], lvl[:], const_sb[:, RANK:RANK + 1], 1.0, ALU.mult, ALU.mult).then_inc(pool_step, 1)
            pool.wait_ge(pool_step, 8)

            def lower(s, j):
                pool.wait_ge(w_hi_ready, s * M + (j + 1))
                nc.gpsimd.tensor_tensor(w_lo[:, ring(s, j), :], slots[:, j % M, :], w_hi[:, ring(s, j), :].bitcast(F32),
                                        ALU.subtract).then_inc(w_lo_pool, 1)

            def weighted_sources(s, i):
                pool.wait_ge(hot_is, s * 2 + (i + 1))
                nc.gpsimd.tensor_tensor(src_hot[:], src_is[:],
                                        vote_w[:, bass.ds(s * 2 * VC + i * VC, VC)].unsqueeze(2).to_broadcast([P, VC, N]),
                                        ALU.mult).then_inc(hot_ready, 1)

            lower(0, 1)
            with pool.Fori(0, 2) as s:
                lower(s, 3)
                lower(s, 5)
                weighted_sources(s, 0)
                lower(s, 8)
                lower(s, 10)
                lower(s, 12)
                weighted_sources(s, 1)
                lower(s, 14)
                lower(s, 17)

            def shifted(n):
                g = ORDER[n]
                heads = slice(g * HG, (g + 1) * HG)
                pool.wait_ge(s_max, n + 1)
                nc.gpsimd.tensor_tensor(att[:, heads, :], att[:, heads, :],
                                        smax[:, heads].unsqueeze(2).to_broadcast([N, HG, N]),
                                        ALU.subtract).then_inc(s_shift, 1)

            def normalized(n):
                g = ORDER[n]
                heads = slice(g * HG, (g + 1) * HG)
                pool.wait_ge(s_inv, n + 1)
                nc.gpsimd.tensor_tensor(att[:, heads, :], att[:, heads, :],
                                        rsm[:, heads].unsqueeze(2).to_broadcast([N, HG, N]),
                                        ALU.mult).then_inc(s_att, 1)

            lower(2, 3)
            lower(2, 5)
            lower(2, 7)
            lower(2, 9)
            lower(2, 10)
            shifted(0)
            shifted(1)
            lower(2, 12)
            shifted(2)
            shifted(3)
            normalized(0)
            normalized(1)
            normalized(2)
            normalized(3)
            lower(2, 17)
            lower(2, 19)
            lower(2, 21)
            pool.wait_ge(s_bo, 16)
            nc.gpsimd.tensor_tensor(x[:], x[:], bo_sb[:], ALU.add).then_inc(s_xb, 1)
            for j in range(C):
                pool.wait_ge(landed[C + j], 64)
                nc.gpsimd.tensor_scalar(w_bf[:, j, :], slots[:, C + j, :].bitcast(I32), -1.0, 1.0, ALU.add,
                                        ALU.mult).then_inc(s_wbf, 1)

        @block.scalar
        def _(act):
            act.dma_start(const_sb[:], const).then_inc(s_const, 16)
            act.dma_start(edges_sb[:], edges).then_inc(s_edges, 16)
            act.dma_start(small_sb[:], small).then_inc(s_small, 16)

            def upper(s, j):
                act.wait_ge(landed[j % M], s * 16 + (16 * (j // M) + 16))
                if ring(s, 0) == ring(s, RL):
                    if j == AHEAD or j >= RL:
                        act.wait_ge(w_used, s * M + j + 1 - (RL - R if j >= RL else 0))
                else:
                    act.wait_ge(w_used, s * M + (j + 1))
                nc.scalar.activation(w_hi[:, ring(s, j), :], slots[:, j % M, :], ACT.Copy).then_inc(w_hi_ready, 1)

            def to_nat(s, i, dst):
                act.wait_ge(w_used, s * M + (R + SC * (i + 1)))
                nc.scalar.activation(dst, proj_ps[0:N, i % 2, :], ACT.Copy).then_inc(nat_ready, 1)

            def fetch_votes(s, i):
                act.wait_ge(votes_done, s * 2 + (i + 1))
                act.wait_ge(votes_kept, s * 6 + (3 * i + 3))
                for g in (0, 2):
                    cols = 4 * N if g == 0 else 2 * N
                    nc.scalar.activation(new_votes[:, g:g + 2, :, :, :].rearrange("p g b a n -> p g (b a n)")[:, :, 0:cols],
                                         mid[0:N, g:g + 2, 0:cols], ACT.Copy).then_inc(votes_read, 1)

            act.wait_ge(dve_step, 1)
            nc.scalar.activation(warm[:, 1:2], warm[:, 0:1], ACT.Sqrt)
            act.wait_ge(s_var, 1)
            nc.scalar.activation(ln[:, 14:15], ln[:, 13:14], ACT.Sqrt, bias=warm[0:N, 0:1]).then_inc(s_std, 1)
            upper(0, 0)
            for h in range(2):
                act.wait_ge(s_xn_turned, h + 1)
                nc.scalar.activation(xn_hi[:, 4 * h:4 * h + 4, :], four(turn_ps[:, h, 0:4 * N]), ACT.Copy).then_inc(s_xn_hi, 1)
            upper(0, 1)
            upper(0, 2)
            act.wait_ge(s_etw, 1)
            nc.scalar.activation(wsp[:, 1, :], wsp[:, 0, :], ACT.Exp, scale=-1.0).then_inc(act_step, 1)
            act.wait_ge(act_step, 1)
            nc.scalar.activation(wsp[:, 2, :], wsp[:, 1, :], ACT.Ln, bias=1.0).then_inc(act_step, 1)
            with act.Fori(0, 2) as s:
                for j in range(AHEAD, M + AHEAD):
                    upper(s, j)
                    if j % SC == 2:
                        i = j // SC - 1
                        to_nat(s, i, nat[:, i % 2, :])
                    if j == 11:
                        fetch_votes(s, 0)
                    if j == 17:
                        fetch_votes(s, 1)

            def exponentials(n):
                g = ORDER[n]
                act.wait_ge(s_shift, n + 1)
                nc.scalar.activation(att[:, g * HG:(g + 1) * HG, :], att[:, g * HG:(g + 1) * HG, :],
                                     ACT.Exp).then_inc(s_exp, 1)

            def att_copy(n):
                g = ORDER[n]
                act.wait_ge(s_att_turned, n + 1)
                nc.scalar.activation(att_t[:, g * HG:(g + 1) * HG, :], four(mid[0:N, g, 0:4 * N]),
                                     ACT.Copy).then_inc(s_att_t, 1)

            for j in range(AHEAD, M + C):
                upper(2, j)
                if j in (18, 20):
                    att_copy(j - 18)
                    att_copy(j - 17)
                if j in NAT_AFTER:
                    i = NAT_AFTER.index(j)
                    to_nat(2, i, nat[:, i, :] if i < 2 else v2[:, (i - 2) * W:(i - 1) * W])
                if j == 9:
                    nc.scalar.activation(warm[:, 1:2], warm[:, 0:1], ACT.Exp)
                if j in (12, 15):
                    exponentials((j - 12) // 3 * 2)
                    exponentials((j - 12) // 3 * 2 + 1)
            nc.scalar.activation(warm[:, 1:2], warm[:, 0:1], ACT.Sqrt)
            act.wait_ge(s_var, 2)
            nc.scalar.activation(ln[:, 30:31], ln[:, 29:30], ACT.Sqrt).then_inc(s_std, 1)

        @block.tensor
        def _(pe):
            for u in range(T):
                if u == 0:
                    pe.wait_ge(s_const, 16)
                if u % 4 == 0:
                    pe.wait_ge(s_xn, u // 4 + 1)
                mm = nc.tensor.transpose(turn_ps[:, u // 4, (u % 4) * N:(u % 4 + 1) * N], xn[:, u * P:(u + 1) * P],
                                         ident[0:N, 0:N])
                if u % 4 == 3:
                    mm.then_inc(s_xn_turned, 1)

            def project(s, j, x_hi, x_lo):
                h, kk = j // SC % 2, j % SC
                if kk == 0:
                    pe.wait_ge(nat_ready, s * 4 + (j // SC + 1))
                by_pool, count = lower_count(s, j)
                pe.wait_ge(w_lo_pool if by_pool else w_lo_dve, count)
                for i in range(2):
                    k = 2 * kk + i
                    cols = slice(i * W, (i + 1) * W)
                    terms = ((x_lo, w_hi), (x_hi, w_lo), (x_hi, w_hi))
                    for t, (xs, ws) in enumerate(terms):
                        mm = nc.tensor.matmul(proj_ps[0:N, h, :], xs[:, k, :], ws[:, ring(s, j), cols],
                                              start=(k == 0 and t == 0), stop=(k == T - 1 and t == 2))
                mm.then_inc(w_used, 1)

            def turn(s, i):
                pe.wait_ge(nat_ready, s * 4 + (2 + i + 1))
                pe.wait_ge(full_ready, s * 4 + (i + 1))
                for u in range(4):
                    mm = nc.tensor.transpose(turn_ps[:, i % 2, u * N:(u + 1) * N], nat[:, i % 2, u * P:(u + 1) * P],
                                             ident[0:N, 0:N])
                mm.then_inc(turned, 1)

            def votes(s, i):
                pe.wait_ge(hot_ready, s * 2 + (i + 1))
                pe.wait_ge(votes_read, s * 4 + (2 * i + 2))
                for c in range(VC):
                    step, pair = c // 2, c % 2
                    for g in range(2):
                        part = slice(EG * g, EG * g + EG)
                        bk = 2 * (step // 2) + g
                        col = (2 * (step % 2) + pair) * N
                        mm = nc.tensor.matmul(mid[0:N, bk, col:col + N], src_hot[part, c, :], dst_hot[part, c, :],
                                              start=True, stop=True)
                mm.then_inc(votes_done, 1)

            pe.sem_inc(w_used, R)
            pe.sem_inc(nat_ready, 2)
            pe.sem_inc(full_ready, 2)
            pe.sem_inc(votes_read, 2)
            for j in range(AHEAD):
                if j % 2 == 0:
                    pe.wait_ge(s_xn_lo, j // 2 + 1)
                project(0, j, xn_hi, xn_lo)
            with pe.Fori(0, 2) as s:
                for j in range(AHEAD, M + AHEAD):
                    if j in (C, C + 2):
                        pe.wait_ge(act_ready, s * 2 + ((j - C) // 2 + 1))
                    if C <= j < M:
                        project(s, j, act_hi, act_lo)
                    else:
                        project(s, j, xn_hi, xn_lo)
                    if j in TURN_AFTER:
                        turn(s, TURN_AFTER.index(j))
                    if j == 7:
                        votes(s, 0)
                    if j == 14:
                        votes(s, 1)

            def scores(n):
                g = ORDER[n]
                for i in range(HG):
                    par, u = g // 2, (g % 2) * HG + i
                    part = slice(D * par, D * par + D)
                    mm = nc.tensor.matmul(mid[0:N, g, i * N:(i + 1) * N], qk2[part, u, :], qk2[part, T + u, :],
                                          start=True, stop=True)
                mm.then_inc(s_scores, 1)

            def att_turn(n):
                g = ORDER[n]
                pe.wait_ge(s_att, n + 1)
                for i in range(HG):
                    mm = nc.tensor.transpose(mid[0:N, g, i * N:(i + 1) * N], att[:, g * HG + i, :],
                                             ident[0:N, 0:N])
                mm.then_inc(s_att_turned, 1)

            def weighted_values(half):
                pe.wait_ge(nat_ready, 2 + 10 + half + 1)
                pe.wait_ge(full_ready, 10 + half + 1)
                pe.wait_ge(s_att_t, 2 * half + 2)
                for u in range(4 * half, 4 * half + 4):
                    for par in range(2):
                        h = 2 * u + par
                        a = (2 * par + u // HG) * HG + u % HG
                        mm = nc.tensor.matmul(turn_ps[D * par:D * par + D, half, (u % 4) * N:(u % 4 + 1) * N],
                                              v2[:, h * D:(h + 1) * D], att_t[:, a, :], start=True, stop=True)
                mm.then_inc(turned, 1)

            for j in range(AHEAD, M + C):
                if j in (C, C + 2):
                    pe.wait_ge(act_ready, 2 * 2 + (j - C) // 2 + 1)
                if j in (M, M + 2):
                    pe.wait_ge(act_ready, 3 * 2 + (j - M) // 2 + 1)
                if j < C:
                    project(2, j, xn_hi, xn_lo)
                elif j < M:
                    project(2, j, act_hi, act_lo)
                else:
                    project(2, j, out_hi, out_lo)
                if j in TURN_AFTER[:2]:
                    turn(2, TURN_AFTER.index(j))
                if j == 5:
                    pe.wait_ge(full_ready, 2 + 8)
                    pe.wait_ge(votes_read, 10)
                    scores(0)
                    scores(1)
                if j == 6:
                    scores(2)
                    scores(3)
                if j in (13, 15):
                    att_turn(j - 13)
                    att_turn(j - 12)
                if j == 14:
                    weighted_values(0)
                if j == 16:
                    weighted_values(1)
            pe.wait_ge(s_row, 16)
            pe.wait_ge(pool_step, 1)
            pe.wait_ge(s_att_t, 4)
            for h in range(2):
                nc.tensor.matmul(mid[0:N, h, :], ones[:], bias_row[:, h * W:(h + 1) * W],
                                 start=True, stop=True).then_inc(s_bias, 1)
            for u in range(T):
                if u % 4 == 0:
                    pe.wait_ge(s_xi, u // 4 + 1)
                mm = nc.tensor.transpose(turn_ps[:, u // 4, (u % 4) * N:(u % 4 + 1) * N], xn[:, u * P:(u + 1) * P],
                                         ident[0:N, 0:N])
                if u % 4 == 3:
                    mm.then_inc(s_xi_turned, 1)
            pe.wait_ge(s_x1, 2)
            for h in range(2):
                for c in range(SC):
                    j = SC * h + c
                    pe.wait_ge(s_wbf, j + 1)
                    for i in range(2):
                        k = 2 * c + i
                        if h == 0 and k % 4 == 0:
                            pe.wait_ge(s_xi_t, k // 4 + 1)
                        mm = nc.tensor.matmul(proj_ps[0:N, h, :], xi_t[:, k, :], w_bf[:, j, i * W:(i + 1) * W],
                                              start=(k == 0), stop=(k == T - 1))
                mm.then_inc(s_ffn, 1)

        @block.vector
        def _(dve):
            steps = [0]

            def step(ins):
                steps[0] += 1
                ins.then_inc(dve_step, 1)
                dve.wait_ge(dve_step, steps[0])

            def lower(s, j):
                dve.wait_ge(w_hi_ready, s * M + (j + 1))
                nc.vector.tensor_tensor(w_lo[:, ring(s, j), :], slots[:, j % M, :], w_hi[:, ring(s, j), :].bitcast(F32),
                                        ALU.subtract).then_inc(w_lo_dve, 1)

            def biased(s, i, dst, bias):
                dve.wait_ge(turned, s * 4 + (i + 1))
                nc.vector.tensor_tensor(dst, four(turn_ps[:, i % 2, 0:4 * N]),
                                        small_sb[:, bias].unsqueeze(2).to_broadcast([P, 4, N]),
                                        ALU.add).then_inc(full_ready, 1)

            def operand(s, i, bias, hi, lo):
                h = i % 2
                biased(s, i, full[:, h, :, :], bias)
                dve.wait_ge(full_ready, s * 4 + (2 + i + 1))
                nc.vector.tensor_copy(hi[:, 4 * h:4 * h + 4, :], full[:, h, :, :]).then_inc(act_hi_ready, 1)
                dve.wait_ge(act_hi_ready, s * 2 + (i + 1))
                nc.vector.tensor_tensor(lo[:, 4 * h:4 * h + 4, :], full[:, h, :, :],
                                        hi[:, 4 * h:4 * h + 4, :].bitcast(F32), ALU.subtract).then_inc(act_ready, 1)

            step(nc.vector.memset(warm[:], LN_EPS))
            dve.wait_ge(s_x, 16)
            nc.vector.bn_stats(ln[:, 0:6], x[:, 0:W])
            step(nc.vector.bn_stats(ln[:, 6:12], x[:, W:F]))
            nc.vector.bn_aggr(ln[:, 12:14], ln[:, 0:12]).then_inc(s_var, 1)
            dve.wait_ge(s_std, 1)
            step(nc.vector.reciprocal(ln[:, 15:16], ln[:, 14:15]))
            for h in range(2):
                cols = slice(h * W, (h + 1) * W)
                nc.vector.tensor_scalar(xn[:, cols], x[:, cols], ln[:, 12:13], ln[:, 15:16], ALU.subtract,
                                        ALU.mult).then_inc(s_xn, 1)
            lower(0, 0)
            for h in range(2):
                dve.wait_ge(s_xn_hi, h + 1)
                nc.vector.tensor_tensor(xn_lo[:, 4 * h:4 * h + 4, :], four(turn_ps[:, h, 0:4 * N]),
                                        xn_hi[:, 4 * h:4 * h + 4, :].bitcast(F32), ALU.subtract).then_inc(s_xn_lo, 1)

            dve.wait_ge(s_small, 16)
            step(nc.vector.tensor_scalar(wsp[:, 3, :], small_sb[0:N, ETW:ETW + 4], 0.0, None, ALU.max))
            nc.vector.scalar_tensor_tensor(out=wsp[:, 0, :], in0=wsp[:, 3, :], scalar=2.0,
                                           in1=small_sb[0:N, ETW:ETW + 4], op0=ALU.mult,
                                           op1=ALU.subtract).then_inc(s_etw, 1)
            lower(0, 2)
            act_scale = small_sb[0:N, ACTS:ACTS + 1]
            step(nc.vector.tensor_scalar(scl[:, 0:1], act_scale, 1e-5, None, ALU.max))
            step(nc.vector.reciprocal(scl[:, 1:2], scl[:, 0:1]))
            step(nc.vector.tensor_tensor(scl[:, 2:3], act_scale, act_scale, ALU.is_equal))
            step(nc.vector.tensor_scalar(scl[:, 3:4], scl[:, 0:1], BIG, None, ALU.is_lt))
            step(nc.vector.tensor_scalar(scl[:, 4:5], scl[:, 0:1], BIG, None, ALU.min))
            step(nc.vector.tensor_tensor(scl[:, 4:5], scl[:, 4:5], scl[:, 3:4], ALU.mult))
            step(nc.vector.tensor_tensor(scl[:, 4:5], scl[:, 4:5], scl[:, 2:3], ALU.mult))
            dve.wait_ge(s_const, 16)
            step(nc.vector.memset(winner[:], 0.0))
            step(nc.vector.tensor_copy(winner[:, 0, 0, :], const_sb[0:N, DIAG:DIAG + N]))
            dve.sem_inc(votes_kept, 3)
            dve.wait_ge(pool_step, 8)

            def one_hots(s, i):
                nc.vector.tensor_tensor(dst_hot[:], iota.unsqueeze(1).to_broadcast([P, VC, N]),
                                        edges_f[:, bass.ds(s * 2 * VC + (i * VC + EC), VC)].unsqueeze(2).to_broadcast([P, VC, N]),
                                        ALU.is_equal)
                nc.vector.tensor_tensor(src_is[:], iota.unsqueeze(1).to_broadcast([P, VC, N]),
                                        edges_f[:, bass.ds(s * 2 * VC + i * VC, VC)].unsqueeze(2).to_broadcast([P, VC, N]),
                                        ALU.is_equal).then_inc(hot_is, 1)

            def keep_votes(s, i):
                dve.wait_ge(votes_read, s * 4 + (2 * i + 4))
                for b in range(VC // 2):
                    dve.wait_ge(votes_kept, s * 2 * 3 + (3 * i + b + 3))
                    dve.nop(nofuse=True)
                    new = new_votes[:, 2 * (b // 2):2 * (b // 2) + 2, b % 2, :, :]
                    nc.vector.copy_predicated(winner[:], new.bitcast(U32), new).then_inc(votes_kept, 1)

            def layer1_bias(s, i):
                return bass.ds(s * T + 4 * i, 4)

            def layer2_bias(s, i):
                return bass.ds(s * T + (3 * T + 4 * (i - 2)), 4)

            with dve.Fori(0, 2) as s:
                lower(s, 4)
                one_hots(s, 0)
                lower(s, 6)
                lower(s, 7)
                operand(s, 0, layer1_bias(s, 0), act_hi, act_lo)
                lower(s, 9)
                lower(s, 11)
                operand(s, 1, layer1_bias(s, 1), act_hi, act_lo)
                one_hots(s, 1)
                lower(s, 13)
                keep_votes(s, 0)
                lower(s, 15)
                biased(s, 2, qk2[:, bass.ds(s * T, 4), :], layer2_bias(s, 2))
                lower(s, 16)
                lower(s, 18)
                biased(s, 3, qk2[:, bass.ds(s * T + 4, 4), :], layer2_bias(s, 3))
                keep_votes(s, 1)

            def build_mask():
                dve.wait_ge(votes_kept, 15)
                final = winner[:, 0, 0, :]
                dve.nop(nofuse=True)
                for q in range(1, 4):
                    votes = winner[:, q % 2, q // 2, :]
                    step(nc.vector.copy_predicated(final, votes.bitcast(U32), votes))
                step(nc.vector.tensor_scalar(code[:], final.bitcast(U32), 22, None, ALU.logical_shift_right))
                step(nc.vector.tensor_scalar(sixth[:], code[:], 63.5, 1.0 / 6.0, ALU.subtract, ALU.mult))
                step(nc.vector.tensor_scalar(sixth[:], sixth[:], ROUND, ROUND, ALU.add, ALU.subtract))
                step(nc.vector.scalar_tensor_tensor(out=typ[:], in0=sixth[:], scalar=-6.0, in1=code[:],
                                                    op0=ALU.mult, op1=ALU.add))
                nc.vector.memset(mask[:], NO_EDGE)
                dve.wait_ge(act_step, 2)
                step(nc.vector.tensor_tensor(wsp[:, 4, :], wsp[:, 2, :], wsp[:, 3, :], ALU.add))
                for t in range(4):
                    last = nc.vector.tensor_scalar(is_typ[:, t, :], typ[:], 62.0 + t, None, ALU.is_equal)
                step(last)
                for t in range(4):
                    step(nc.vector.copy_predicated(mask[:], is_typ[:, t, :], wsp[:, 4, t:t + 1].to_broadcast([N, N])))

            def masked_scores(n):
                g = ORDER[n]
                heads = slice(g * HG, (g + 1) * HG)
                dve.wait_ge(s_scores, n + 1)
                step(nc.vector.scalar_tensor_tensor(
                    out=att[:, heads, :], in0=four(mid[0:N, g, 0:4 * N]), scalar=SCALE,
                    in1=mask[:].unsqueeze(1).to_broadcast([N, HG, N]), op0=ALU.mult, op1=ALU.add))
                nc.vector.tensor_reduce(smax[:, heads], att[:, heads, :], AX.X, ALU.max).then_inc(s_max, 1)

            def inverse_sums(n):
                g = ORDER[n]
                heads = slice(g * HG, (g + 1) * HG)
                dve.wait_ge(s_exp, n + 1)
                step(nc.vector.tensor_reduce(ssm[:, heads], att[:, heads, :], AX.X, ALU.add))
                nc.vector.reciprocal(rsm[:, heads], ssm[:, heads]).then_inc(s_inv, 1)

            lower(2, 4)
            build_mask()
            lower(2, 6)
            operand(2, 0, slice(2 * T, 2 * T + 4), act_hi, act_lo)
            lower(2, 8)
            masked_scores(0)
            masked_scores(1)
            lower(2, 11)
            operand(2, 1, slice(2 * T + 4, 3 * T), act_hi, act_lo)
            masked_scores(2)
            masked_scores(3)
            lower(2, 13)
            inverse_sums(0)
            inverse_sums(1)
            lower(2, 14)
            inverse_sums(2)
            inverse_sums(3)
            lower(2, 15)
            lower(2, 16)
            operand(2, 2, slice(5 * T, 5 * T + 4), out_hi, out_lo)
            lower(2, 18)
            operand(2, 3, slice(5 * T + 4, 6 * T), out_hi, out_lo)
            lower(2, 20)
            lower(2, 22)
            lower(2, 23)
            dve.wait_ge(s_xb, 1)
            for h in range(2):
                cols = slice(h * W, (h + 1) * W)
                dve.wait_ge(w_used, R + 3 * M + SC * (h + 1))
                nc.vector.tensor_tensor(x1[:, cols], proj_ps[0:N, h, :], x[:, cols], ALU.add).then_inc(s_x1, 1)
                dve.wait_ge(s_x1, h + 1)
                step(nc.vector.bn_stats(ln[:, 16 + 6 * h:22 + 6 * h], x1[:, cols]))
            step(nc.vector.bn_aggr(ln[:, 28:30], ln[:, 16:28]))
            step(nc.vector.tensor_tensor(ln[:, 31:32], ln[:, 29:30], ln[:, 29:30], ALU.is_equal))
            nc.vector.tensor_scalar(ln[:, 29:30], ln[:, 29:30], 0.0, LN_EPS, ALU.max, ALU.add).then_inc(s_var, 1)
            dve.wait_ge(s_std, 2)
            step(nc.vector.reciprocal(ln[:, 15:16], ln[:, 30:31]))
            step(nc.vector.tensor_tensor(ln[:, 15:16], ln[:, 15:16], scl[:, 1:2], ALU.mult))
            for h in range(2):
                cols = slice(h * W, (h + 1) * W)
                step(nc.vector.tensor_scalar(xn[:, cols], x1[:, cols], ln[:, 28:29], ln[:, 15:16], ALU.subtract, ALU.mult))
                step(nc.vector.tensor_scalar(xn[:, cols], xn[:, cols], QB, -QB, ALU.min, ALU.max))
                nc.vector.tensor_scalar(xn[:, cols], xn[:, cols], ln[:, 31:32], ROUND, ALU.mult, ALU.add).then_inc(s_xi, 1)
            for h in range(2):
                dve.wait_ge(s_xi_turned, h + 1)
                nc.vector.tensor_scalar(xi_t[:, 4 * h:4 * h + 4, :], four(turn_ps[:, h, 0:4 * N]), ROUND, None,
                                        ALU.subtract).then_inc(s_xi_t, 1)
            for h in range(2):
                cols = slice(h * W, (h + 1) * W)
                dve.wait_ge(s_bias, h + 1)
                step(nc.vector.tensor_tensor(x1[:, cols], mid[0:N, h, :], x1[:, cols], ALU.add))
            for h in range(2):
                cols = slice(h * W, (h + 1) * W)
                dve.wait_ge(s_ffn, h + 1)
                nc.vector.scalar_tensor_tensor(out=x1[:, cols], in0=proj_ps[0:N, h, :], scalar=scl[:, 4:5],
                                               in1=x1[:, cols], op0=ALU.mult, op1=ALU.add).then_inc(s_fin, 1)


def kernel(x, src, dst, edge_type_5, L0_gnn_edge_type_weights, L0_gnn_wq, L0_gnn_bq, L0_gnn_wk, L0_gnn_bk,
           L0_gnn_wv, L0_gnn_bv, L0_gnn_wiq, L0_gnn_biq, L0_gnn_wik, L0_gnn_bik, L0_gnn_wiv, L0_gnn_biv,
           L0_gnn_wo, L0_gnn_bo, L0_ffn_ternary_weight, L0_ffn_bias, L0_ffn_act_scale):
    import numpy as np
    import concourse.bacc as bacc
    from concourse.bass_utils import run_bass_kernel_spmd

    def chunks(w):
        return np.asarray(w).reshape(2, W, SC, 2, P).transpose(0, 2, 4, 3, 1).reshape(C, P, F)

    def edge_columns(a):
        return np.asarray(a).reshape(2, 2, EC // 2, EG).transpose(1, 3, 2, 0).reshape(P, EC)

    small = np.empty((P, SMALL), np.float32)
    for i, b in enumerate((L0_gnn_bq, L0_gnn_bk, L0_gnn_bv, L0_gnn_biq, L0_gnn_bik, L0_gnn_biv)):
        small[:, BIAS + i * T:BIAS + (i + 1) * T] = np.asarray(b).reshape(T, P).T
    small[:, ETW:ETW + 4] = np.asarray(L0_gnn_edge_type_weights)[None, :]
    small[:, ACTS] = np.asarray(L0_ffn_act_scale)
    const = np.zeros((P, CONST), np.float32)
    const[:, IDENT:IDENT + P] = np.eye(P)
    const[:, IOTA:IOTA + N] = np.arange(N)[None, :]
    const[:, RANK] = 2.0 ** (3.0 * (np.arange(P) % EG) - 96.0)
    const[:N, DIAG:DIAG + N] = np.eye(N) * 3.0 * 2.0 ** -96
    arrays = {
        "in_x": np.asarray(x),
        "in_small": small,
        "in_const": const,
        "in_rows": np.stack([np.asarray(L0_gnn_bo), np.asarray(L0_ffn_bias)]),
        "in_edges": np.ascontiguousarray(np.concatenate([edge_columns(a) for a in (src, dst, edge_type_5)], axis=1)),
        "in_w_proj": np.stack([chunks(w) for w in (L0_gnn_wq, L0_gnn_wiq, L0_gnn_wk, L0_gnn_wik, L0_gnn_wv,
                                                   L0_gnn_wiv, L0_gnn_wo)]),
        "in_w_ternary": np.ascontiguousarray(chunks(L0_ffn_ternary_weight)),
    }
    nc = bacc.Bacc("TRN2", target_bir_lowering=False, num_devices=1)
    aps = [nc.dram_tensor(name, a.shape, mybir.dt.from_np(a.dtype), kind="ExternalInput").ap()
           for name, a in arrays.items()]
    out = nc.dram_tensor("out", (N, F), F32, kind="ExternalOutput").ap()
    gnn_ffn(nc, *aps, out)
    r = run_bass_kernel_spmd(nc, [arrays], core_ids=[0])
    return r.results[0]["out"]
```

```python
from contextlib import ExitStack

import concourse.bass as bass
from concourse import mybir

ALU = mybir.AluOpType
ACT = mybir.ActivationFunctionType
AX = mybir.AxisListType
F32 = mybir.dt.float32
F32R = mybir.dt.float32r
BF16 = mybir.dt.bfloat16
I32 = mybir.dt.int32
U32 = mybir.dt.uint32

P = 128
N = 96
F = 1024
T = F // P
W = 512
H = 16
D = F // H
HG = 4
E = 3072
EG = 64
EC = E // P
C = 8
SC = C // 2
M = 2 * C
R = 4
RL = 6
GROWS = 7
AHEAD, ACT_AHEAD = 3, 4
VC = 6
WAIT_FOR_X, WAIT_FOR_XN, WAIT_FOR_XI = 13, 5, 8
LN_EPS = 1e-5
SCALE = 1.0 / 8.0
QB = 127.0
ROUND = 1.5 * 2.0 ** 23
BIG = 3.0e38
NO_EDGE = -3.0e38
ORDER = (0, 2, 1, 3)

BY_POOL = [1, 3, 5, 8, 10, 12, 14]
BY_DVE = [j for j in range(M) if j not in BY_POOL]
LAST_POOL = [3, 5, 7, 8, 10, 11, 12, 13, 16, 18, 20]
LAST_DVE = [j for j in range(AHEAD, M + C) if j not in LAST_POOL]
TURN_AFTER = (5, 8, 13, 17)

BIAS = 0
ETW = 6 * T
ACTS = ETW + 4
SMALL = ACTS + 1
IDENT = 0
IOTA = IDENT + P
RANK = IOTA + N
DIAG = RANK + 1
CONST = DIAG + N


def is_last(s):
    return isinstance(s, int) and s == 2


def lower_count(s, j):
    for by_pool, mine, in_last in ((True, BY_POOL, LAST_POOL), (False, BY_DVE, LAST_DVE)):
        if is_last(s) and j in in_last:
            return by_pool, 2 * len(mine) + len([c for c in mine if c < AHEAD]) + in_last.index(j) + 1
        if not is_last(s) and j % M in mine:
            return by_pool, s * len(mine) + (j // M * len(mine) + mine.index(j % M) + 1)


def ring(s, j):
    if is_last(s) and j >= GROWS:
        return (4, 5, 3, 0, 1, 2)[(j - GROWS) % RL]
    return j % R


def buffers(s, j):
    if not is_last(s) or j < GROWS:
        return R
    return RL if j >= GROWS + RL - R else None


def gnn_ffn(nc, x_in, small, const, rows, edges, w_proj, w_ternary, out):
    ctx = ExitStack()
    with ctx:
        def sb(name, shape, dt=F32):
            return ctx.enter_context(nc.sbuf_tensor(name, shape, dt))

        def sem(name):
            return ctx.enter_context(nc.semaphore(name))

        slots = sb("slots", [P, M, F])
        w_hi = sb("w_hi", [P, RL, F], F32R)
        w_lo = sb("w_lo", [P, RL, F], F32R)
        w_bf = sb("w_bf", [P, C, F], BF16)

        small_sb = sb("small_sb", [P, SMALL])
        const_sb = sb("const_sb", [P, CONST])
        x = sb("x", [N, F])
        xn = sb("xn", [N, F])
        xn_hi = sb("xn_hi", [P, T, N], F32R)
        xn_lo = sb("xn_lo", [P, T, N], F32R)
        nat = sb("nat", [N, 2, W])
        full = sb("full", [P, 2, 4, N])
        qkv_hi = sb("qkv_hi", [P, T, N], F32R)
        qkv_lo = sb("qkv_lo", [P, T, N], F32R)
        qk2 = sb("qk2", [P, 2 * T, N])
        v2 = sb("v2", [N, F])
        att = sb("att", [N, H, N])
        att_t = sb("att_t", [N, H, N])
        out_hi, out_lo = xn_hi, xn_lo
        x1 = v2
        xi_t = sb("xi_t", [P, T, N], BF16)
        bo_sb = xn
        bias_row = sb("bias_row", [1, F])
        ones = sb("ones", [1, N])
        scratch = sb("scratch", [P, W], BF16)
        ln = sb("ln", [N, 32])
        warm = sb("warm", [P, 4])
        scl = sb("scl", [N, 6])
        neg_max = sb("neg_max", [N, H])
        ssm = sb("ssm", [N, H])
        rsm = sb("rsm", [N, H])
        edges_sb = sb("edges_sb", [P, 3 * EC], I32)
        edges_f = sb("edges_f", [P, 3 * EC])
        typ3 = sb("typ3", [P, EC])
        lvl = sb("lvl", [P, EC])
        vote_w = sb("vote_w", [P, EC])
        src_is = sb("src_is", [P, VC, N], BF16)
        src_hot = sb("src_hot", [P, VC, N], BF16)
        dst_hot = sb("dst_hot", [P, VC, N], BF16)
        new_votes = att[:].rearrange("p (g b a) n -> p g b a n", g=4, b=2)
        winner = sb("winner", [N, 2, 2, N])
        code = sb("code", [N, N], U32)
        sixth = sb("sixth", [N, N])
        typ = sb("typ", [N, N])
        is_typ = sb("is_typ", [N, 4, N], U32)
        mask = sb("mask", [N, N])
        wsp = sb("wsp", [N, 8, 4])

        proj_ps = ctx.enter_context(nc.psum_tensor("proj_ps", [P, 2, W], F32))
        turn_ps = ctx.enter_context(nc.psum_tensor("turn_ps", [P, 2, W], F32))
        mid = ctx.enter_context(nc.psum_tensor("mid", [P, 4, W], F32))

        s_x = sem("s_x")
        s_small = sem("s_small")
        s_const = sem("s_const")
        s_edges = sem("s_edges")
        s_bo = sem("s_bo")
        s_row = sem("s_row")
        landed = [sem(f"landed{j}") for j in range(M)]
        pool_step = sem("pool_step")
        dve_step = sem("dve_step")
        s_var = sem("s_var")
        s_std = sem("s_std")
        s_xn = sem("s_xn")
        s_xn_turned = sem("s_xn_turned")
        s_xn_hi = sem("s_xn_hi")
        s_xn_lo = sem("s_xn_lo")
        w_hi_ready = sem("w_hi_ready")
        w_lo_dve = sem("w_lo_dve")
        w_lo_pool = sem("w_lo_pool")
        w_used = sem("w_used")
        nat_ready = sem("nat_ready")
        turned = sem("turned")
        full_ready = sem("full_ready")
        operand_hi_ready = sem("operand_hi_ready")
        operand_ready = sem("operand_ready")
        hot_is = sem("hot_is")
        hot_ready = sem("hot_ready")
        votes_done = sem("votes_done")
        votes_read = sem("votes_read")
        votes_kept = sem("votes_kept")
        s_etw = sem("s_etw")
        s_exp_w = sem("s_exp_w")
        s_scores = sem("s_scores")
        s_max = sem("s_max")
        s_exp = sem("s_exp")
        s_inv = sem("s_inv")
        s_att = sem("s_att")
        s_att_turned = sem("s_att_turned")
        s_att_t = sem("s_att_t")
        s_xb = sem("s_xb")
        s_x1 = sem("s_x1")
        s_bias = sem("s_bias")
        s_wbf = sem("s_wbf")
        s_xi = sem("s_xi")
        s_xi_turned = sem("s_xi_turned")
        s_xi_t = sem("s_xi_t")
        s_ffn = sem("s_ffn")
        s_fin = sem("s_fin")
        s_out = sem("s_out")

        ident = const_sb[:, IDENT:IDENT + P]
        iota = const_sb[:, IOTA:IOTA + N]

        def four(ap):
            return ap.rearrange("p (t n) -> p t n", t=4)

        block = ctx.enter_context(nc.Block())

        @block.sync
        def _(sp):
            sp.dma_start(x[:], x_in).then_inc(s_x, 16)
            sp.dma_start(const_sb[:], const).then_inc(s_const, 16)
            for j in range(M):
                if j == 1:
                    sp.dma_start(edges_sb[:], edges).then_inc(s_edges, 16)
                sp.dma_start(slots[:, j, :], w_proj[j // C, j % C]).then_inc(landed[j], 16)
            with sp.Fori(1, 3) as s:
                for j in range(M):
                    sp.wait_ge(w_used, s * M + (R + j + 1 - M))
                    sp.dma_start(slots[:, j, :], w_proj[bass.ds(s * 2 + j // C, 1), j % C].rearrange(
                        "a p c -> p (a c)")).then_inc(landed[j], 16)
            for j in range(C):
                sp.wait_ge(w_used, R + 2 * M + j + 1)
                sp.dma_start(slots[:, j, :], w_proj[6, j]).then_inc(landed[j], 16)
            sp.dma_start(bo_sb[:], rows[0:1, :].to_broadcast([N, F])).then_inc(s_bo, 16)
            sp.dma_start(bias_row[:], rows[1:2, :]).then_inc(s_row, 16)
            for j in range(C, M):
                sp.wait_ge(w_used, R + 2 * M + j + 1)
                sp.dma_start(slots[:, j, :].bitcast(I32), w_ternary[j - C]).then_inc(landed[j], 16)
            for h in range(2):
                sp.wait_ge(s_fin, h + 1)
                sp.dma_start(out[:, h * W:(h + 1) * W], x1[:, h * W:(h + 1) * W]).then_inc(s_out, 16)
            sp.wait_ge(s_out, 32)

        @block.gpsimd
        def _(pool):
            nc.gpsimd.memset(scratch[:], 0.0)
            nc.gpsimd.memset(winner[:], 0.0)
            nc.gpsimd.memset(mask[:], NO_EDGE)
            nc.gpsimd.memset(ones[:], 1.0).then_inc(pool_step, 1)
            pool.wait_ge(s_edges, 16)
            nc.gpsimd.tensor_copy(edges_f[:], edges_sb[:]).then_inc(pool_step, 1)
            etype = edges_f[:, 2 * EC:3 * EC]
            pool.wait_ge(pool_step, 2)
            nc.gpsimd.tensor_scalar(typ3[:], etype, 4.0, 0.5, ALU.is_equal, ALU.mult).then_inc(pool_step, 1)
            nc.gpsimd.tensor_scalar(lvl[:], etype, 0.0, 2.5, ALU.is_equal, ALU.mult).then_inc(pool_step, 1)
            nc.gpsimd.tensor_scalar(vote_w[:], etype, 0.5, 0.5, ALU.mult, ALU.add).then_inc(pool_step, 1)
            pool.wait_ge(pool_step, 5)
            nc.gpsimd.tensor_tensor(lvl[:], lvl[:], typ3[:], ALU.add).then_inc(pool_step, 1)
            pool.wait_ge(pool_step, 6)
            nc.gpsimd.tensor_tensor(lvl[:], lvl[:], vote_w[:], ALU.add).then_inc(pool_step, 1)
            pool.wait_ge(pool_step, 7)
            pool.wait_ge(s_const, 16)
            nc.gpsimd.tensor_scalar(vote_w[:], lvl[:], const_sb[:, RANK:RANK + 1], 1.0, ALU.mult, ALU.mult).then_inc(pool_step, 1)
            pool.wait_ge(pool_step, 8)

            def lower(s, j):
                pool.wait_ge(w_hi_ready, s * M + (j + 1))
                nc.gpsimd.tensor_tensor(w_lo[:, ring(s, j), :], slots[:, j % M, :], w_hi[:, ring(s, j), :].bitcast(F32),
                                        ALU.subtract).then_inc(w_lo_pool, 1)

            def weighted_sources(s, i):
                pool.wait_ge(hot_is, s * 2 + (i + 1))
                nc.gpsimd.tensor_tensor(src_hot[:], src_is[:],
                                        vote_w[:, bass.ds(s * 2 * VC + i * VC, VC)].unsqueeze(2).to_broadcast([P, VC, N]),
                                        ALU.mult).then_inc(hot_ready, 1)

            lower(0, 1)
            lower(0, 3)
            with pool.Fori(0, 2) as s:
                lower(s, 5)
                lower(s, 8)
                lower(s, 10)
                weighted_sources(s, 0)
                lower(s, 12)
                lower(s, 14)
                weighted_sources(s, 1)
                lower(s, 17)
                lower(s, 19)

            def normalized(n):
                g = ORDER[n]
                heads = slice(g * HG, (g + 1) * HG)
                pool.wait_ge(s_inv, n + 1)
                nc.gpsimd.tensor_tensor(att[:, heads, :], att[:, heads, :],
                                        rsm[:, heads].unsqueeze(2).to_broadcast([N, HG, N]),
                                        ALU.mult).then_inc(s_att, 1)

            lower(2, 5)
            lower(2, 7)
            lower(2, 8)
            lower(2, 10)
            lower(2, 11)
            lower(2, 12)
            lower(2, 13)
            normalized(0)
            normalized(1)
            lower(2, 16)
            normalized(2)
            normalized(3)
            lower(2, 18)
            lower(2, 20)
            pool.wait_ge(s_bo, 16)
            nc.gpsimd.tensor_tensor(x[:], x[:], bo_sb[:], ALU.add).then_inc(s_xb, 1)
            for j in range(C):
                pool.wait_ge(landed[C + j], 64)
                nc.gpsimd.tensor_scalar(w_bf[:, j, :], slots[:, C + j, :].bitcast(I32), -1.0, 1.0, ALU.add,
                                        ALU.mult).then_inc(s_wbf, 1)

        @block.scalar
        def _(act):
            act.dma_start(small_sb[:], small).then_inc(s_small, 16)

            def upper(s, j):
                act.wait_ge(landed[j % M], s * 16 + (16 * (j // M) + 16))
                if buffers(s, j):
                    act.wait_ge(w_used, s * M + (R + j + 1 - buffers(s, j)))
                nc.scalar.activation(w_hi[:, ring(s, j), :], slots[:, j % M, :], ACT.Copy).then_inc(w_hi_ready, 1)

            def to_nat(s, i, dst):
                act.wait_ge(w_used, s * M + (R + SC * (i + 1)))
                nc.scalar.activation(dst, proj_ps[0:N, i % 2, :], ACT.Copy).then_inc(nat_ready, 1)

            def fetch_votes(s, i):
                act.wait_ge(votes_done, s * 2 + (i + 1))
                act.wait_ge(votes_kept, s * 6 + (3 * i + 3))
                for g in (0, 2):
                    cols = 4 * N if g == 0 else 2 * N
                    nc.scalar.activation(new_votes[:, g:g + 2, :, :, :].rearrange("p g b a n -> p g (b a n)")[:, :, 0:cols],
                                         mid[0:N, g:g + 2, 0:cols], ACT.Copy).then_inc(votes_read, 1)

            act.wait_ge(dve_step, 1)
            nc.scalar.activation(warm[:, 1:2], warm[:, 0:1], ACT.Sqrt)
            act.wait_ge(s_var, 1)
            nc.scalar.activation(ln[:, 14:15], ln[:, 13:14], ACT.Sqrt, bias=warm[0:N, 0:1]).then_inc(s_std, 1)
            act.wait_ge(s_etw, 1)
            nc.scalar.activation(wsp[:, 1, :], wsp[:, 0, :], ACT.Exp, scale=-1.0).then_inc(s_exp_w, 1)
            upper(0, 0)
            for h in range(2):
                act.wait_ge(s_xn_turned, h + 1)
                nc.scalar.activation(xn_hi[:, 4 * h:4 * h + 4, :], four(turn_ps[:, h, 0:4 * N]), ACT.Copy).then_inc(s_xn_hi, 1)
            for j in range(1, ACT_AHEAD):
                upper(0, j)
            with act.Fori(0, 2) as s:
                for j in range(ACT_AHEAD, M + ACT_AHEAD):
                    upper(s, j)
                    if j % SC == 2:
                        i = j // SC - 1
                        to_nat(s, i, nat[:, i % 2, :])
                    if j == 14:
                        fetch_votes(s, 0)
                fetch_votes(s, 1)

            def exponentials(n):
                act.wait_ge(s_max, n + 1)
                for a in range(ORDER[n] * HG, (ORDER[n] + 1) * HG):
                    last = nc.scalar.activation(att[:, a, :], att[:, a, :], ACT.Exp, bias=neg_max[:, a:a + 1],
                                                accum_out=ssm[:, a:a + 1])
                last.then_inc(s_exp, 1)

            def att_copy(n):
                g = ORDER[n]
                act.wait_ge(s_att_turned, n + 1)
                nc.scalar.activation(att_t[:, g * HG:(g + 1) * HG, :], four(mid[0:N, g, 0:4 * N]),
                                     ACT.Copy).then_inc(s_att_t, 1)

            for j in range(ACT_AHEAD, M + C):
                upper(2, j)
                if j == 7:
                    to_nat(2, 0, nat[:, 0, :])
                if j == 12:
                    to_nat(2, 1, nat[:, 1, :])
                if j == 15:
                    exponentials(0)
                    exponentials(1)
                if j == 16:
                    exponentials(2)
                    to_nat(2, 2, v2[:, 0:W])
                    att_copy(0)
                    att_copy(1)
                    exponentials(3)
                if j == 18:
                    att_copy(2)
                    att_copy(3)
                    to_nat(2, 3, v2[:, W:F])
            nc.scalar.activation(warm[:, 3:4], warm[:, 0:1], ACT.Sqrt)
            act.wait_ge(s_var, 2)
            nc.scalar.activation(ln[:, 30:31], ln[:, 14:15], ACT.Sqrt).then_inc(s_std, 1)

        @block.tensor
        def _(pe):
            def keep_clock(n):
                for _ in range(n):
                    nc.tensor.matmul(mid[0:N, 3, :], scratch[:, 0:N], scratch[:], start=True, stop=True)

            pe.wait_ge(pool_step, 1)
            keep_clock(WAIT_FOR_X)
            for u in range(T):
                if u == 0:
                    pe.wait_ge(s_const, 16)
                if u % 4 == 0:
                    pe.wait_ge(s_xn, u // 4 + 1)
                mm = nc.tensor.transpose(turn_ps[:, u // 4, (u % 4) * N:(u % 4 + 1) * N], xn[:, u * P:(u + 1) * P],
                                         ident[0:N, 0:N])
                if u % 4 == 3:
                    mm.then_inc(s_xn_turned, 1)

            keep_clock(WAIT_FOR_XN)

            def project(s, j, x_hi, x_lo):
                h, kk = j // SC % 2, j % SC
                if kk == 0:
                    pe.wait_ge(nat_ready, s * 4 + (j // SC + 1))
                by_pool, count = lower_count(s, j)
                pe.wait_ge(w_lo_pool if by_pool else w_lo_dve, count)
                for i in range(2):
                    k = 2 * kk + i
                    cols = slice(i * W, (i + 1) * W)
                    terms = ((x_lo, w_hi), (x_hi, w_lo), (x_hi, w_hi))
                    for t, (xs, ws) in enumerate(terms):
                        mm = nc.tensor.matmul(proj_ps[0:N, h, :], xs[:, k, :], ws[:, ring(s, j), cols],
                                              start=(k == 0 and t == 0), stop=(k == T - 1 and t == 2))
                mm.then_inc(w_used, 1)

            def turn(s, i):
                pe.wait_ge(nat_ready, s * 4 + (2 + i + 1))
                pe.wait_ge(full_ready, s * 4 + (i + 1))
                for u in range(4):
                    mm = nc.tensor.transpose(turn_ps[:, i % 2, u * N:(u + 1) * N], nat[:, i % 2, u * P:(u + 1) * P],
                                             ident[0:N, 0:N])
                mm.then_inc(turned, 1)

            def votes(s, i):
                pe.wait_ge(hot_ready, s * 2 + (i + 1))
                pe.wait_ge(votes_read, s * 4 + (2 * i + 2))
                for c in range(VC):
                    step, pair = c // 2, c % 2
                    for g in range(2):
                        part = slice(EG * g, EG * g + EG)
                        bk = 2 * (step // 2) + g
                        col = (2 * (step % 2) + pair) * N
                        mm = nc.tensor.matmul(mid[0:N, bk, col:col + N], src_hot[part, c, :], dst_hot[part, c, :],
                                              start=True, stop=True)
                mm.then_inc(votes_done, 1)

            pe.sem_inc(w_used, R)
            pe.sem_inc(nat_ready, 2)
            pe.sem_inc(full_ready, 2)
            pe.sem_inc(votes_read, 2)
            for j in range(AHEAD):
                if j % 2 == 0:
                    pe.wait_ge(s_xn_lo, j // 2 + 1)
                project(0, j, xn_hi, xn_lo)
            with pe.Fori(0, 2) as s:
                for j in range(AHEAD, M + AHEAD):
                    if j in (C, C + 2):
                        pe.wait_ge(operand_ready, s * 2 + ((j - C) // 2 + 1))
                    if C <= j < M:
                        project(s, j, qkv_hi, qkv_lo)
                    else:
                        project(s, j, xn_hi, xn_lo)
                    if j in TURN_AFTER:
                        turn(s, TURN_AFTER.index(j))
                    if j == 11:
                        votes(s, 0)
                    if j == 15:
                        votes(s, 1)

            def scores(n):
                g = ORDER[n]
                for i in range(HG):
                    par, u = g // 2, (g % 2) * HG + i
                    part = slice(D * par, D * par + D)
                    mm = nc.tensor.matmul(mid[0:N, g, i * N:(i + 1) * N], qk2[part, u, :], qk2[part, T + u, :],
                                          start=True, stop=True)
                mm.then_inc(s_scores, 1)

            def att_turn(n):
                g = ORDER[n]
                pe.wait_ge(s_att, n + 1)
                for i in range(HG):
                    mm = nc.tensor.transpose(mid[0:N, g, i * N:(i + 1) * N], att[:, g * HG + i, :],
                                             ident[0:N, 0:N])
                mm.then_inc(s_att_turned, 1)

            def weighted_values(half):
                pe.wait_ge(nat_ready, 2 + 10 + half + 1)
                pe.wait_ge(full_ready, 10 + half + 1)
                pe.wait_ge(s_att_t, 2 * half + 2)
                for u in range(4 * half, 4 * half + 4):
                    for par in range(2):
                        h = 2 * u + par
                        a = (2 * par + u // HG) * HG + u % HG
                        mm = nc.tensor.matmul(turn_ps[D * par:D * par + D, half, (u % 4) * N:(u % 4 + 1) * N],
                                              v2[:, h * D:(h + 1) * D], att_t[:, a, :], start=True, stop=True)
                mm.then_inc(turned, 1)

            for j in range(AHEAD, M + C):
                if j in (C, C + 2):
                    pe.wait_ge(operand_ready, 2 * 2 + (j - C) // 2 + 1)
                if j in (M, M + 2):
                    pe.wait_ge(operand_ready, 3 * 2 + (j - M) // 2 + 1)
                if j < C:
                    project(2, j, xn_hi, xn_lo)
                elif j < M:
                    project(2, j, qkv_hi, qkv_lo)
                else:
                    project(2, j, out_hi, out_lo)
                if j in TURN_AFTER[:2]:
                    turn(2, TURN_AFTER.index(j))
                if j == 5:
                    pe.wait_ge(full_ready, 2 + 8)
                    pe.wait_ge(votes_read, 10)
                    scores(0)
                    scores(1)
                if j == 6:
                    scores(2)
                    scores(3)
                if j in (13, 15):
                    att_turn(j - 13)
                    att_turn(j - 12)
                if j == 14:
                    weighted_values(0)
                if j == 16:
                    weighted_values(1)
            pe.wait_ge(s_row, 16)
            pe.wait_ge(s_att_t, 4)
            for h in range(2):
                nc.tensor.matmul(mid[0:N, h, :], ones[:], bias_row[:, h * W:(h + 1) * W],
                                 start=True, stop=True).then_inc(s_bias, 1)
            keep_clock(WAIT_FOR_XI)
            for u in range(T):
                if u % 4 == 0:
                    pe.wait_ge(s_xi, u // 4 + 1)
                mm = nc.tensor.transpose(turn_ps[:, u // 4, (u % 4) * N:(u % 4 + 1) * N], xn[:, u * P:(u + 1) * P],
                                         ident[0:N, 0:N])
                if u % 4 == 3:
                    mm.then_inc(s_xi_turned, 1)
            pe.wait_ge(s_x1, 2)
            for h in range(2):
                for c in range(SC):
                    j = SC * h + c
                    pe.wait_ge(s_wbf, j + 1)
                    for i in range(2):
                        k = 2 * c + i
                        if h == 0 and k % 4 == 0:
                            pe.wait_ge(s_xi_t, k // 4 + 1)
                        mm = nc.tensor.matmul(proj_ps[0:N, h, :], xi_t[:, k, :], w_bf[:, j, i * W:(i + 1) * W],
                                              start=(k == 0), stop=(k == T - 1))
                mm.then_inc(s_ffn, 1)

        @block.vector
        def _(dve):
            steps = [0]

            def step(ins):
                steps[0] += 1
                ins.then_inc(dve_step, 1)
                dve.wait_ge(dve_step, steps[0])

            def lower(s, j):
                dve.wait_ge(w_hi_ready, s * M + (j + 1))
                nc.vector.tensor_tensor(w_lo[:, ring(s, j), :], slots[:, j % M, :], w_hi[:, ring(s, j), :].bitcast(F32),
                                        ALU.subtract).then_inc(w_lo_dve, 1)

            def biased(s, i, dst, bias):
                dve.wait_ge(turned, s * 4 + (i + 1))
                nc.vector.tensor_tensor(dst, four(turn_ps[:, i % 2, 0:4 * N]),
                                        small_sb[:, bias].unsqueeze(2).to_broadcast([P, 4, N]),
                                        ALU.add).then_inc(full_ready, 1)

            def operand(s, i, bias, hi, lo):
                h = i % 2
                biased(s, i, full[:, h, :, :], bias)
                dve.wait_ge(full_ready, s * 4 + (2 + i + 1))
                nc.vector.tensor_copy(hi[:, 4 * h:4 * h + 4, :], full[:, h, :, :]).then_inc(operand_hi_ready, 1)
                dve.wait_ge(operand_hi_ready, s * 2 + (i + 1))
                nc.vector.tensor_tensor(lo[:, 4 * h:4 * h + 4, :], full[:, h, :, :],
                                        hi[:, 4 * h:4 * h + 4, :].bitcast(F32), ALU.subtract).then_inc(operand_ready, 1)

            step(nc.vector.memset(warm[:], LN_EPS))
            dve.wait_ge(s_x, 16)
            nc.vector.bn_stats(ln[:, 0:6], x[:, 0:W])
            step(nc.vector.bn_stats(ln[:, 6:12], x[:, W:F]))
            nc.vector.bn_aggr(ln[:, 12:14], ln[:, 0:12]).then_inc(s_var, 1)
            dve.wait_ge(s_small, 16)
            step(nc.vector.tensor_scalar(wsp[:, 3, :], small_sb[0:N, ETW:ETW + 4], 0.0, None, ALU.max))
            nc.vector.scalar_tensor_tensor(out=wsp[:, 0, :], in0=wsp[:, 3, :], scalar=2.0,
                                           in1=small_sb[0:N, ETW:ETW + 4], op0=ALU.mult,
                                           op1=ALU.subtract).then_inc(s_etw, 1)
            dve.wait_ge(s_std, 1)
            step(nc.vector.reciprocal(ln[:, 15:16], ln[:, 14:15]))
            for h in range(2):
                cols = slice(h * W, (h + 1) * W)
                nc.vector.tensor_scalar(xn[:, cols], x[:, cols], ln[:, 12:13], ln[:, 15:16], ALU.subtract,
                                        ALU.mult).then_inc(s_xn, 1)
            lower(0, 0)
            for h in range(2):
                dve.wait_ge(s_xn_hi, h + 1)
                nc.vector.tensor_tensor(xn_lo[:, 4 * h:4 * h + 4, :], four(turn_ps[:, h, 0:4 * N]),
                                        xn_hi[:, 4 * h:4 * h + 4, :].bitcast(F32), ALU.subtract).then_inc(s_xn_lo, 1)

            lower(0, 2)
            lower(0, 4)
            e, z, zz, poly = wsp[:, 1, :], wsp[:, 5, :], wsp[:, 6, :], wsp[:, 7, :]
            dve.wait_ge(s_exp_w, 1)
            step(nc.vector.tensor_scalar(wsp[:, 2, :], e, 2.0, None, ALU.add))
            step(nc.vector.reciprocal(wsp[:, 2, :], wsp[:, 2, :]))
            step(nc.vector.tensor_tensor(z, e, wsp[:, 2, :], ALU.mult))
            step(nc.vector.tensor_tensor(zz, z, z, ALU.mult))
            step(nc.vector.tensor_scalar(poly, zz, 1.0 / 15.0, None, ALU.mult))
            for n in (13.0, 11.0, 9.0, 7.0, 5.0, 3.0):
                step(nc.vector.scalar_tensor_tensor(out=poly, in0=poly, scalar=1.0 / n, in1=zz, op0=ALU.add, op1=ALU.mult))
            step(nc.vector.scalar_tensor_tensor(out=poly, in0=poly, scalar=1.0, in1=z, op0=ALU.add, op1=ALU.mult))
            step(nc.vector.scalar_tensor_tensor(out=wsp[:, 4, :], in0=poly, scalar=2.0, in1=wsp[:, 3, :],
                                                op0=ALU.mult, op1=ALU.add))
            dve.wait_ge(s_const, 16)
            dve.wait_ge(pool_step, 1)
            step(nc.vector.tensor_copy(winner[:, 0, 0, :], const_sb[0:N, DIAG:DIAG + N]))
            dve.sem_inc(votes_kept, 3)
            dve.wait_ge(pool_step, 8)

            def one_hots(s, i):
                if i == 1:
                    dve.wait_ge(votes_done, s * 2 + 1)
                nc.vector.tensor_tensor(dst_hot[:], iota.unsqueeze(1).to_broadcast([P, VC, N]),
                                        edges_f[:, bass.ds(s * 2 * VC + (i * VC + EC), VC)].unsqueeze(2).to_broadcast([P, VC, N]),
                                        ALU.is_equal)
                nc.vector.tensor_tensor(src_is[:], iota.unsqueeze(1).to_broadcast([P, VC, N]),
                                        edges_f[:, bass.ds(s * 2 * VC + i * VC, VC)].unsqueeze(2).to_broadcast([P, VC, N]),
                                        ALU.is_equal).then_inc(hot_is, 1)

            def keep_votes(s, i):
                dve.wait_ge(votes_read, s * 4 + (2 * i + 4))
                for b in range(VC // 2):
                    dve.wait_ge(votes_kept, s * 2 * 3 + (3 * i + b + 3))
                    dve.nop(nofuse=True)
                    new = new_votes[:, 2 * (b // 2):2 * (b // 2) + 2, b % 2, :, :]
                    nc.vector.copy_predicated(winner[:], new.bitcast(U32), new).then_inc(votes_kept, 1)

            def layer1_bias(s, i):
                return bass.ds(s * T + 4 * i, 4)

            def layer2_bias(s, i):
                return bass.ds(s * T + (3 * T + 4 * (i - 2)), 4)

            lower(0, 6)
            with dve.Fori(0, 2) as s:
                lower(s, 7)
                operand(s, 0, layer1_bias(s, 0), qkv_hi, qkv_lo)
                one_hots(s, 0)
                lower(s, 9)
                operand(s, 1, layer1_bias(s, 1), qkv_hi, qkv_lo)
                lower(s, 11)
                lower(s, 13)
                one_hots(s, 1)
                lower(s, 15)
                lower(s, M)
                biased(s, 2, qk2[:, bass.ds(s * T, 4), :], layer2_bias(s, 2))
                keep_votes(s, 0)
                lower(s, M + 2)
                lower(s, M + 4)
                biased(s, 3, qk2[:, bass.ds(s * T + 4, 4), :], layer2_bias(s, 3))
                lower(s, M + 6)
                keep_votes(s, 1)

            def build_mask():
                dve.wait_ge(votes_kept, 15)
                final = winner[:, 0, 0, :]
                dve.nop(nofuse=True)
                for q in range(1, 4):
                    votes = winner[:, q % 2, q // 2, :]
                    step(nc.vector.copy_predicated(final, votes.bitcast(U32), votes))
                step(nc.vector.tensor_scalar(code[:], final.bitcast(U32), 22, None, ALU.logical_shift_right))
                step(nc.vector.tensor_scalar(sixth[:], code[:], 63.5, 1.0 / 6.0, ALU.subtract, ALU.mult))
                step(nc.vector.tensor_scalar(sixth[:], sixth[:], ROUND, ROUND, ALU.add, ALU.subtract))
                step(nc.vector.scalar_tensor_tensor(out=typ[:], in0=sixth[:], scalar=-6.0, in1=code[:],
                                                    op0=ALU.mult, op1=ALU.add))
                for t in range(4):
                    last = nc.vector.tensor_scalar(is_typ[:, t, :], typ[:], 62.0 + t, None, ALU.is_equal)
                step(last)
                for t in range(4):
                    step(nc.vector.copy_predicated(mask[:], is_typ[:, t, :], wsp[:, 4, t:t + 1].to_broadcast([N, N])))

            def masked_scores(n):
                g = ORDER[n]
                heads = slice(g * HG, (g + 1) * HG)
                dve.wait_ge(s_scores, n + 1)
                step(nc.vector.scalar_tensor_tensor(
                    out=att[:, heads, :], in0=four(mid[0:N, g, 0:4 * N]), scalar=SCALE,
                    in1=mask[:].unsqueeze(1).to_broadcast([N, HG, N]), op0=ALU.mult, op1=ALU.add))
                nc.vector.tensor_reduce(neg_max[:, heads], att[:, heads, :], AX.X, ALU.max,
                                        negate=True).then_inc(s_max, 1)

            def inverse_sums(n):
                g = ORDER[n]
                heads = slice(g * HG, (g + 1) * HG)
                dve.wait_ge(s_exp, n + 1)
                nc.vector.reciprocal(rsm[:, heads], ssm[:, heads]).then_inc(s_inv, 1)

            build_mask()
            operand(2, 0, slice(2 * T, 2 * T + 4), qkv_hi, qkv_lo)
            lower(2, 9)
            operand(2, 1, slice(2 * T + 4, 3 * T), qkv_hi, qkv_lo)
            masked_scores(0)
            masked_scores(1)
            masked_scores(2)
            inverse_sums(0)
            masked_scores(3)
            inverse_sums(1)
            lower(2, 14)
            inverse_sums(2)
            lower(2, 15)
            inverse_sums(3)
            operand(2, 2, slice(5 * T, 5 * T + 4), out_hi, out_lo)
            lower(2, 17)
            operand(2, 3, slice(5 * T + 4, 6 * T), out_hi, out_lo)
            lower(2, 19)
            lower(2, 21)
            lower(2, 22)
            lower(2, 23)
            act_scale = small_sb[0:N, ACTS:ACTS + 1]
            step(nc.vector.tensor_scalar(scl[:, 0:1], act_scale, 1e-5, None, ALU.max))
            step(nc.vector.reciprocal(scl[:, 1:2], scl[:, 0:1]))
            step(nc.vector.tensor_tensor(scl[:, 2:3], act_scale, act_scale, ALU.is_equal))
            step(nc.vector.tensor_scalar(scl[:, 3:4], scl[:, 0:1], BIG, None, ALU.is_lt))
            step(nc.vector.tensor_scalar(scl[:, 4:5], scl[:, 0:1], BIG, None, ALU.min))
            step(nc.vector.tensor_tensor(scl[:, 4:5], scl[:, 4:5], scl[:, 3:4], ALU.mult))
            step(nc.vector.tensor_tensor(scl[:, 4:5], scl[:, 4:5], scl[:, 2:3], ALU.mult))
            dve.wait_ge(s_xb, 1)
            for h in range(2):
                cols = slice(h * W, (h + 1) * W)
                dve.wait_ge(w_used, R + 3 * M + SC * (h + 1))
                nc.vector.tensor_tensor(x1[:, cols], proj_ps[0:N, h, :], x[:, cols], ALU.add).then_inc(s_x1, 1)
                dve.wait_ge(s_x1, h + 1)
                step(nc.vector.bn_stats(ln[:, 16 + 6 * h:22 + 6 * h], x1[:, cols]))
            step(nc.vector.bn_aggr(ln[:, 28:30], ln[:, 16:28]))
            nc.vector.tensor_scalar(ln[:, 14:15], ln[:, 29:30], 0.0, LN_EPS, ALU.max, ALU.add).then_inc(s_var, 1)
            step(nc.vector.tensor_tensor(ln[:, 31:32], ln[:, 29:30], ln[:, 29:30], ALU.is_equal))
            step(nc.vector.tensor_scalar(ln[:, 12:13], ln[:, 31:32], QB, None, ALU.mult))
            step(nc.vector.tensor_scalar(ln[:, 13:14], ln[:, 31:32], -QB, None, ALU.mult))
            dve.wait_ge(s_std, 2)
            step(nc.vector.reciprocal(ln[:, 15:16], ln[:, 30:31]))
            step(nc.vector.tensor_tensor(ln[:, 15:16], ln[:, 15:16], scl[:, 1:2], ALU.mult))
            for h in range(2):
                cols = slice(h * W, (h + 1) * W)
                step(nc.vector.tensor_scalar(xn[:, cols], x1[:, cols], ln[:, 28:29], ln[:, 15:16], ALU.subtract, ALU.mult))
                nc.vector.tensor_scalar(xn[:, cols], xn[:, cols], ln[:, 12:13], ln[:, 13:14], ALU.min,
                                        ALU.max).then_inc(s_xi, 1)
            for h in range(2):
                dve.wait_ge(s_xi_turned, h + 1)
                nc.vector.tensor_scalar(xi_t[:, 4 * h:4 * h + 4, :], four(turn_ps[:, h, 0:4 * N]), ROUND, ROUND,
                                        ALU.add, ALU.subtract).then_inc(s_xi_t, 1)
            for h in range(2):
                cols = slice(h * W, (h + 1) * W)
                dve.wait_ge(s_bias, h + 1)
                step(nc.vector.tensor_tensor(x1[:, cols], mid[0:N, h, :], x1[:, cols], ALU.add))
            for h in range(2):
                cols = slice(h * W, (h + 1) * W)
                dve.wait_ge(s_ffn, h + 1)
                nc.vector.scalar_tensor_tensor(out=x1[:, cols], in0=proj_ps[0:N, h, :], scalar=scl[:, 4:5],
                                               in1=x1[:, cols], op0=ALU.mult, op1=ALU.add).then_inc(s_fin, 1)


def kernel(x, src, dst, edge_type_5, L0_gnn_edge_type_weights, L0_gnn_wq, L0_gnn_bq, L0_gnn_wk, L0_gnn_bk,
           L0_gnn_wv, L0_gnn_bv, L0_gnn_wiq, L0_gnn_biq, L0_gnn_wik, L0_gnn_bik, L0_gnn_wiv, L0_gnn_biv,
           L0_gnn_wo, L0_gnn_bo, L0_ffn_ternary_weight, L0_ffn_bias, L0_ffn_act_scale):
    import numpy as np
    import concourse.bacc as bacc
    from concourse.bass_utils import run_bass_kernel_spmd

    def chunks(w):
        return np.asarray(w).reshape(2, W, SC, 2, P).transpose(0, 2, 4, 3, 1).reshape(C, P, F)

    def edge_columns(a):
        return np.asarray(a).reshape(2, 2, EC // 2, EG).transpose(1, 3, 2, 0).reshape(P, EC)

    small = np.empty((P, SMALL), np.float32)
    for i, b in enumerate((L0_gnn_bq, L0_gnn_bk, L0_gnn_bv, L0_gnn_biq, L0_gnn_bik, L0_gnn_biv)):
        small[:, BIAS + i * T:BIAS + (i + 1) * T] = np.asarray(b).reshape(T, P).T
    small[:, ETW:ETW + 4] = np.asarray(L0_gnn_edge_type_weights)[None, :]
    small[:, ACTS] = np.asarray(L0_ffn_act_scale)
    const = np.zeros((P, CONST), np.float32)
    const[:, IDENT:IDENT + P] = np.eye(P)
    const[:, IOTA:IOTA + N] = np.arange(N)[None, :]
    const[:, RANK] = 2.0 ** (3.0 * (np.arange(P) % EG) - 96.0)
    const[:N, DIAG:DIAG + N] = np.eye(N) * 3.0 * 2.0 ** -96
    arrays = {
        "in_x": np.asarray(x),
        "in_small": small,
        "in_const": const,
        "in_rows": np.stack([np.asarray(L0_gnn_bo), np.asarray(L0_ffn_bias)]),
        "in_edges": np.ascontiguousarray(np.concatenate([edge_columns(a) for a in (src, dst, edge_type_5)], axis=1)),
        "in_w_proj": np.stack([chunks(w) for w in (L0_gnn_wq, L0_gnn_wiq, L0_gnn_wk, L0_gnn_wik, L0_gnn_wv,
                                                   L0_gnn_wiv, L0_gnn_wo)]),
        "in_w_ternary": np.ascontiguousarray(chunks(L0_ffn_ternary_weight)),
    }
    nc = bacc.Bacc("TRN2", target_bir_lowering=False, num_devices=1)
    aps = [nc.dram_tensor(name, a.shape, mybir.dt.from_np(a.dtype), kind="ExternalInput").ap()
           for name, a in arrays.items()]
    out = nc.dram_tensor("out", (N, F), F32, kind="ExternalOutput").ap()
    gnn_ffn(nc, *aps, out)
    r = run_bass_kernel_spmd(nc, [arrays], core_ids=[0])
    return r.results[0]["out"]
```
